# Optimizing a Trainium2 kernel written in Bass

```python
import numpy as np
import jax
import jax.numpy as jnp

def _softmax(x, axis=-1):
    return jax.nn.softmax(x, axis=axis)

def _gelu(x):
    return jax.nn.gelu(x, approximate=True)

def _silu(x):
    return jax.nn.silu(x)

def _sigmoid(x):
    return jax.nn.sigmoid(x)

def _layernorm(x, axis=-1, eps=1e-05):
    m = jnp.mean(x, axis=axis, keepdims=True)
    v = jnp.var(x, axis=axis, keepdims=True)
    return (x - m) / jnp.sqrt(v + eps)

def _scatter_add(tgt, idx, src, axis=0):
    return tgt.at[idx].add(src)

def _segment_sum(src, seg, n):
    return jax.ops.segment_sum(src, seg, n)
kernel_name = 'mk_gnn_resnorm_d4_gnn_r32_472ecc'

def setup_inputs(seed: int=0):
    np.random.seed(seed)
    _w = jnp.asarray

    def _rec_inputs():
        import jax
        import jax.numpy as jnp
        _gk = jax.random.key(seed)
        x = -0.000202 + 1 * jax.random.normal(jax.random.fold_in(_gk, 1), (3125, 64), jnp.float32)
        src = jax.random.randint(jax.random.fold_in(_gk, 2), (100000,), 0, 3125, jnp.int32)
        dst = jax.random.randint(jax.random.fold_in(_gk, 3), (100000,), 0, 3125, jnp.int32)
        _o = jnp.argsort(dst, stable=True)
        src = src[_o]
        dst = dst[_o]
        edge_attr_32 = 0.000196303 + 1.00016 * jax.random.normal(jax.random.fold_in(_gk, 12), (100000, 32), jnp.float32)
        return (x, src, dst, edge_attr_32)
    x, src, dst, edge_attr_32 = _rec_inputs()

    def _L0_gnn_setup():
        import jax, jax.numpy as jnp
        import numpy as np
        K_LAYERS = 10
        ALPHA = 0.1
        N_NODES = 3125
        N_EDGES = 50000
        D_FEAT = 64
        key = jax.random.key(seed)
        k1, k2, k3 = jax.random.split(key, 3)
        features = jax.random.normal(k1, (N_NODES, D_FEAT), dtype=jnp.float32)
        src = jax.random.randint(k2, (N_EDGES,), 0, N_NODES, dtype=jnp.int64)
        dst = jax.random.randint(k3, (N_EDGES,), 0, N_NODES, dtype=jnp.int64)
        return {'features': features, 'src': src, 'dst': dst}
    _L0_gnn_all = _L0_gnn_setup()
    _L0_gnn_in = {k: v for k, v in _L0_gnn_all.items() if k in ()}
    del _L0_gnn_all

    def _L1_gnn_setup():
        import jax, jax.numpy as jnp
        import numpy as np
        N_NODES = 50000
        N_EDGES = 25000
        D_IN = 64
        D_OUT = 64
        EDGE_DIM = 32
        BN_EPS = 1e-05
        GIN_EPS = 0.0
        key = jax.random.key(seed)
        ks = jax.random.split(key, 8)
        x = jax.random.normal(ks[0], (N_NODES, D_IN), dtype=jnp.float32)
        edge_index = jax.random.randint(ks[1], (2, N_EDGES), 0, N_NODES, dtype=jnp.int64)
        edge_attr = jax.random.normal(ks[2], (N_EDGES, EDGE_DIM), dtype=jnp.float32)
        We = jax.random.normal(ks[3], (EDGE_DIM, D_IN), dtype=jnp.float32) / np.sqrt(EDGE_DIM)
        be = jnp.zeros((D_IN,), dtype=jnp.float32)
        W1 = jax.random.normal(ks[4], (D_IN, D_OUT), dtype=jnp.float32) / np.sqrt(D_IN)
        b1 = jnp.zeros((D_OUT,), dtype=jnp.float32)
        gamma = jnp.ones((D_OUT,), dtype=jnp.float32)
        beta = jnp.zeros((D_OUT,), dtype=jnp.float32)
        W2 = jax.random.normal(ks[5], (D_OUT, D_OUT), dtype=jnp.float32) / np.sqrt(D_OUT)
        b2 = jnp.zeros((D_OUT,), dtype=jnp.float32)
        return {'x': x, 'edge_index': edge_index, 'edge_attr': edge_attr, 'We': We, 'be': be, 'W1': W1, 'b1': b1, 'gamma': gamma, 'beta': beta, 'W2': W2, 'b2': b2}
    _L1_gnn_all = _L1_gnn_setup()
    _L1_gnn_in = {k: v for k, v in _L1_gnn_all.items() if k in ('We', 'be', 'W1', 'b1', 'gamma', 'beta', 'W2', 'b2')}
    del _L1_gnn_all

    def _L2_gnn_setup():
        import jax, jax.numpy as jnp
        import numpy as np
        N_NODES = 3125
        N_EDGES = 50000
        IN_FEATS = 64
        OUT_FEATS = 64
        K_HOPS = 2
        key = jax.random.key(seed)
        k1, k2, k3, k4, k5, k6, k7 = jax.random.split(key, 7)
        feat = jax.random.normal(k1, (N_NODES, IN_FEATS), dtype=jnp.float32)
        src = jax.random.randint(k2, (N_EDGES,), 0, N_NODES, dtype=jnp.int64)
        dst = jax.random.randint(k3, (N_EDGES,), 0, N_NODES, dtype=jnp.int64)
        s = 1.0 / np.sqrt(IN_FEATS)
        W = jax.random.uniform(k4, (OUT_FEATS, IN_FEATS), jnp.float32, -s, s)
        b = jax.random.uniform(k5, (OUT_FEATS,), jnp.float32, -s, s)
        Wr = jax.random.uniform(k6, (OUT_FEATS, IN_FEATS), jnp.float32, -s, s)
        br = jax.random.uniform(k7, (OUT_FEATS,), jnp.float32, -s, s)
        return {'feat': feat, 'W': W, 'b': b, 'Wr': Wr, 'br': br, 'src': src, 'dst': dst}
    _L2_gnn_all = _L2_gnn_setup()
    _L2_gnn_in = {k: v for k, v in _L2_gnn_all.items() if k in ('W', 'b', 'Wr', 'br')}
    del _L2_gnn_all

    def _L3_gnn_setup():
        import jax, jax.numpy as jnp
        import numpy as np
        DIM = 64
        HEADS = 4
        N_NODES = 50000
        N_EDGES = 25000
        NEG_SLOPE = 0.2
        key = jax.random.key(seed)
        k1, k2, k3, k4, k5 = jax.random.split(key, 5)
        meta_x = jax.random.normal(k1, (N_NODES, DIM), dtype=jnp.float32)
        meta_edge_index = jax.random.randint(k2, (2, N_EDGES), 0, N_NODES, dtype=jnp.int64)
        glorot = float(np.sqrt(2.0 / (DIM + HEADS * DIM)))
        W = jax.random.normal(k3, (DIM, HEADS * DIM), dtype=jnp.float32) * glorot
        att_src = jax.random.normal(k4, (1, HEADS, DIM), dtype=jnp.float32) * glorot
        att_dst = jax.random.normal(k5, (1, HEADS, DIM), dtype=jnp.float32) * glorot
        bias = jnp.zeros((DIM,), dtype=jnp.float32)
        return {'meta_x': meta_x, 'meta_edge_index': meta_edge_index, 'W': W, 'att_src': att_src, 'att_dst': att_dst, 'bias': bias}
    _L3_gnn_all = _L3_gnn_setup()
    _L3_gnn_in = {k: v for k, v in _L3_gnn_all.items() if k in ('W', 'att_src', 'att_dst', 'bias')}
    del _L3_gnn_all
    return {'x': x, 'src': src, 'dst': dst, 'edge_attr_32': edge_attr_32, 'L1_gnn_We': _L1_gnn_in['We'], 'L1_gnn_be': _L1_gnn_in['be'], 'L1_gnn_W1': _L1_gnn_in['W1'], 'L1_gnn_b1': _L1_gnn_in['b1'], 'L1_gnn_gamma': _L1_gnn_in['gamma'], 'L1_gnn_beta': _L1_gnn_in['beta'], 'L1_gnn_W2': _L1_gnn_in['W2'], 'L1_gnn_b2': _L1_gnn_in['b2'], 'L2_gnn_W': _L2_gnn_in['W'], 'L2_gnn_b': _L2_gnn_in['b'], 'L2_gnn_Wr': _L2_gnn_in['Wr'], 'L2_gnn_br': _L2_gnn_in['br'], 'L3_gnn_W': _L3_gnn_in['W'], 'L3_gnn_att_src': _L3_gnn_in['att_src'], 'L3_gnn_att_dst': _L3_gnn_in['att_dst'], 'L3_gnn_bias': _L3_gnn_in['bias']}

def reference(x, src, dst, edge_attr_32, L1_gnn_We, L1_gnn_be, L1_gnn_W1, L1_gnn_b1, L1_gnn_gamma, L1_gnn_beta, L1_gnn_W2, L1_gnn_b2, L2_gnn_W, L2_gnn_b, L2_gnn_Wr, L2_gnn_br, L3_gnn_W, L3_gnn_att_src, L3_gnn_att_dst, L3_gnn_bias):
    import jax
    import jax.numpy as jnp

    def _L0_gnn_ref(features, src, dst):
        import jax, jax.numpy as jnp
        import numpy as np
        K_LAYERS = 10
        ALPHA = 0.1
        N_NODES = 3125
        N_EDGES = 50000
        D_FEAT = 64
        n = features.shape[0]
        ones = jnp.ones((src.shape[0],), dtype=features.dtype)
        deg_out = jax.ops.segment_sum(ones, src, num_segments=n)
        deg_in = jax.ops.segment_sum(ones, dst, num_segments=n)
        norm_src = jnp.clip(deg_out, 1.0) ** (-0.5)
        norm_dst = jnp.clip(deg_in, 1.0) ** (-0.5)
        h0 = features
        h = features
        for _ in range(K_LAYERS):
            msg = (h * norm_src[:, None])[src]
            agg = jax.ops.segment_sum(msg, dst, num_segments=n)
            h = (1.0 - ALPHA) * (agg * norm_dst[:, None]) + ALPHA * h0
        return h

    def _L1_gnn_ref(x, edge_index, edge_attr, We, be, W1, b1, gamma, beta, W2, b2):
        import jax, jax.numpy as jnp
        import numpy as np
        N_NODES = 50000
        N_EDGES = 25000
        D_IN = 64
        D_OUT = 64
        EDGE_DIM = 32
        BN_EPS = 1e-05
        GIN_EPS = 0.0
        src = edge_index[0]
        dst = edge_index[1]
        msg = x[src] + (edge_attr @ We + be)
        agg = jax.ops.segment_sum(msg, dst, num_segments=x.shape[0])
        out = agg + (1.0 + GIN_EPS) * x
        h = out @ W1 + b1
        mean = jnp.mean(h, axis=0)
        var = jnp.var(h, axis=0)
        h = (h - mean) * jax.lax.rsqrt(var + BN_EPS) * gamma + beta
        h = jax.nn.relu(h)
        return h @ W2 + b2

    def _L2_gnn_ref(feat, W, b, Wr, br, src, dst):
        import jax, jax.numpy as jnp
        import numpy as np
        N_NODES = 3125
        N_EDGES = 50000
        IN_FEATS = 64
        OUT_FEATS = 64
        K_HOPS = 2
        n = feat.shape[0]
        deg = jax.ops.segment_sum(jnp.ones_like(dst, dtype=feat.dtype), dst, num_segments=n)
        inv_sqrt = jnp.where(deg > 0, deg, 1.0) ** (-0.5)
        h = feat
        for _ in range(K_HOPS):
            h = h * inv_sqrt[:, None]
            msg = h[src]
            h = jax.ops.segment_sum(msg, dst, num_segments=n)
            h = h * inv_sqrt[:, None]
        out = h @ W.T + b
        out = out + feat @ Wr.T + br
        return out

    def _L3_gnn_ref(meta_x, meta_edge_index, W, att_src, att_dst, bias):
        import jax, jax.numpy as jnp
        import numpy as np
        DIM = 64
        HEADS = 4
        N_NODES = 50000
        N_EDGES = 25000
        NEG_SLOPE = 0.2
        N = meta_x.shape[0]
        loops = jnp.arange(N, dtype=meta_edge_index.dtype)
        edge = jnp.concatenate([meta_edge_index, jnp.stack([loops, loops])], axis=1)
        src, dst = (edge[0], edge[1])
        x = (meta_x @ W).reshape(N, HEADS, DIM)
        a_src = jnp.sum(x * att_src, axis=-1)
        a_dst = jnp.sum(x * att_dst, axis=-1)
        logits = a_src[src] + a_dst[dst]
        logits = jax.nn.leaky_relu(logits, NEG_SLOPE)
        seg_max = jax.ops.segment_max(logits, dst, num_segments=N)
        ex = jnp.exp(logits - seg_max[dst])
        seg_sum = jax.ops.segment_sum(ex, dst, num_segments=N)
        alpha = ex / (seg_sum[dst] + 1e-16)
        msg = x[src] * alpha[:, :, None]
        out = jax.ops.segment_sum(msg, dst, num_segments=N)
        return out.mean(axis=1) + bias
    edge_index = jnp.stack([src, dst])
    x = _layernorm(x + _L0_gnn_ref(x, src, dst), axis=-1)
    x = _layernorm(x + _L1_gnn_ref(x, edge_index, edge_attr_32, L1_gnn_We, L1_gnn_be, L1_gnn_W1, L1_gnn_b1, L1_gnn_gamma, L1_gnn_beta, L1_gnn_W2, L1_gnn_b2), axis=-1)
    x = _layernorm(x + _L2_gnn_ref(x, L2_gnn_W, L2_gnn_b, L2_gnn_Wr, L2_gnn_br, src, dst), axis=-1)
    x = _layernorm(x + _L3_gnn_ref(x, edge_index, L3_gnn_W, L3_gnn_att_src, L3_gnn_att_dst, L3_gnn_bias), axis=-1)
    return x

_drawn_inputs = setup_inputs


def setup_inputs(seed=0):
    import zlib

    import numpy as np

    out = dict(_drawn_inputs(seed))
    spreads = {'L1_gnn_be': (0.0, 0.278),
     'L1_gnn_b1': (0.0, 0.8),
     'L1_gnn_gamma': (1.0, 0.2),
     'L1_gnn_beta': (0.0, 0.1),
     'L1_gnn_b2': (0.0, 0.1),
     'L3_gnn_bias': (0.0, 0.1)}
    factors = {'L3_gnn_att_src': 3.429, 'L3_gnn_att_dst': 8.0}
    for name, (base, spread) in spreads.items():
        noise = np.random.default_rng([zlib.crc32(name.encode()), seed]).standard_normal(out[name].shape)
        drawn = base * np.exp(spread * noise) if base else spread * noise
        out[name] = jnp.asarray(drawn.astype(out[name].dtype))
    for name, factor in factors.items():
        out[name] = (out[name] * factor).astype(out[name].dtype)
    return out
```

```python
from contextlib import ExitStack
import concourse.bass as bass
from concourse import mybir

ALU = mybir.AluOpType
ACT = mybir.ActivationFunctionType
AX = mybir.AxisListType.X
F32 = mybir.dt.float32
F16 = mybir.dt.float16
I32 = mybir.dt.int32

P = 128
LO = 2048.0


class Count:

    def __init__(self, eng, sem):
        self.eng, self.sem, self.n, self.base = eng, sem, 0, 0

    def add(self, ins):
        ins.then_inc(self.sem, 1)
        self.n += 1
        return ins

    def here(self):
        self.eng.wait_ge(self.sem, self.base + self.n)

    def loop(self, i, per):
        self.base, self.n0, self.per = i * per, self.n, per

    def end(self, times):
        assert self.n - self.n0 == self.per, (self.n - self.n0, self.per)
        self.base, self.n = 0, self.n0 + self.per * times


def gnn_kernel(nc, x, dst, edges, We, be, W1, b1, gamma, beta, W2, b2, Wl, bl, Wr, br, Wg, att_s, att_d, bias_g, out):
    N, D = x.shape
    E = dst.shape[0]
    DE = edges.shape[1] - 2
    T = -(-N // P)
    W = 13
    K = 4
    WG = 11
    G = 22
    SLOT = P * K
    NW = W * WG * G
    ROW = 160
    R = E // ROW
    NC = WG * K
    KEY = T * W
    EC = K * (DE + 2)
    H = att_s.shape[1]
    TP = T * P
    BL = [(t, min(4, T - t)) for t in range(0, T, 4)]
    NB = len(BL)
    HOPS = 10
    EPS = 1e-5
    LAST = N - (T - 1) * P
    XS = 256.0
    S1 = D + 1
    RB = 5

    with ExitStack() as ctx:
        def sb(name, shape, dt):
            return ctx.enter_context(nc.sbuf_tensor(name, shape, dt))

        def ps(name, shape, dt=F32):
            return ctx.enter_context(nc.psum_tensor(name, shape, dt))

        def sem(name):
            return ctx.enter_context(nc.semaphore(name))

        starts_d = nc.dram_tensor("starts_d", (256,), I32)
        C = sb("C", [P, T, TP], F16)
        eaT = sb("eaT", [65, TP], F32)
        starts_row = sb("starts_row", [1, 256], I32)
        dego = sb("dego", [P, T], F32)
        ones = sb("ones", [1, P], F32)
        first_f = eaT[0:1, 0:R]
        ident = sb("ident", [P, P], F32)
        ident16 = sb("ident16", [P, P], F16)
        row64 = sb("row64", [S1, 1], F32)
        eps_c = sb("eps_c", [P, 1], F32)
        weS = sb("weS", [S1, D], F32)
        w1 = sb("w1", [D, D], F32)
        w2 = sb("w2", [S1, D], F32)
        vecs = sb("vecs", [D, 3], F32)
        wlr = sb("wlr", [D, 2 * D], F32)
        wlrT = sb("wlrT", [P, D], F32)
        wg = sb("wg", [D, H, D], F32)
        wa = sb("wa", [D, 2, H], F32)
        nwa = sb("nwa", [D, H], F32)
        biases = sb("biases", [P, 3, D], F32)
        nrm = sb("nrm", [P, 12, T], F32)
        small = sb("small", [P, 64], F32)
        mv = sb("mv", [P, 4, 2], F32)
        sd = sb("sd", [P, 4], F32)
        with ExitStack() as built:
            def bb(name, shape, dt):
                return built.enter_context(nc.sbuf_tensor(name, shape, dt))

            iota_p = bb("iota_p", [P, P], F16)
            iota_key = bb("iota_key", [P, T, W], F16)
            iota_j = bb("iota_j", [P, W, NC], F16)
            iota_t = bb("iota_t", [P, T, NC], F16)
            woff = bb("woff", [P, WG, K], F32)
            with ExitStack() as search:
                def tb(name, shape, dt):
                    return search.enter_context(nc.sbuf_tensor(name, shape, dt))

                fb = tb("fb", [P, R], F32)
                fs = tb("fs", [P, R], F32)
                wlo = tb("wlo", [P, 2], F32)
                cnt = tb("cnt", [P, 8], F32)
                row_i = tb("row_i", [P, 2], I32)
                rows_i = tb("rows_i", [P, 2, ROW], I32)
                st_i = tb("st_i", [P, 2], I32)
            raw = bb("raw", [P, 2, WG, EC], I32)
            ohp = bb("ohp", [P, 2, K, P], F16)
            ohk = bb("ohk", [P, 2, K, KEY], F16)
            ohj = bb("ohj", [P, 2, W, NC], F16)
            oht = bb("oht", [P, 2, T, NC], F16)
            eahl = bb("eahl", [P, NC, 2 * DE + 1], F16)
            ki = bb("ki", [P, 2, WG, K], I32)
            kf = bb("kf", [P, 5, WG, K], F32)
            dl16 = bb("dl16", [P, 2, WG, K], F16)
            tv16 = bb("tv16", [P, WG, K], F16)

        xs = sb("xs", [P, T, D], F32)
        with ExitStack() as layers:
            def lb(name, shape, dt):
                return layers.enter_context(nc.sbuf_tensor(name, shape, dt))

            GH = lb("GH", [P, 2, T, 2 * D], F16)
            plo = lb("plo", [P, 2, 4, D], F32)
            S = lb("S", [P, 2, 4, D], F32)
            V = lb("V", [P, 2, 4, D], F32)
            xc = lb("xc", [P, 2, 4, D], F32)
            z = lb("z", [P, 2, 4, 2 * D], F32)
            zT = lb("zT", [P, 2, 4 * P], F32)
            bst = lb("bst", [D, NB, 6], F32)
            bnv = lb("bnv", [D, 8], F32)
        F = sb("F", [P, T, 4 * S1], F16)
        acc = sb("acc", [P, T, D], F32)
        Mr = sb("Mr", [P, RB, 4 * P], F16)
        Vg = sb("Vg", [P, 2, 4, S1], F32)
        Vd = sb("Vd", [P, 2, 4, S1], F32)
        r1 = Vg[:].rearrange("p e n c -> p (e n c)").rearrange("p (n c) -> p n c", c=2 * S1)
        c2 = Vd[:].rearrange("p e n c -> p (e n c)").rearrange("p (n c) -> p n c", c=2 * S1)
        q = sb("q", [P, 4, S1], F32)
        rd = sb("rd", [P, 4], F32)
        heads = sb("heads", [P, H, 5, T], F32)
        hd = sb("hd", [P, 5, T], F32)
        asad = acc[:].rearrange("p t d -> p (t d)")[:, 0:2 * H * T].rearrange("p (e h t) -> p e h t", e=2, h=H)
        att = z[0:D].rearrange("p s n c -> p (s n c)")[:, 0:2 * H * D].rearrange("p (e h d) -> p e h d", e=2, h=H)
        wadb = sb("wadb", [D, P], F32)
        wgh = sb("wgh", [D, D], F32)
        amax = sb("amax", [P, 2, H], F32)
        bank = ps("bank", [P, 8, 512])
        pk = [bank[:, i] for i in range(2)]
        pdeg = [bank[:, 2 + i] for i in range(2)]
        pea = [bank[:, 4 + i] for i in range(2)]
        pf = bank[:, 6:8].rearrange("p a b -> p (a b)")

        s_first = sem("s_first")
        s_firstf = sem("s_firstf")
        s_firstb = sem("s_firstb")
        s_iota = sem("s_iota")
        s_ones = sem("s_ones")
        s_rowidx = sem("s_rowidx")
        s_rows = sem("s_rows")
        s_start = sem("s_start")
        s_startd = sem("s_startd")
        s_startrow = sem("s_startrow")
        s_raw = [sem(f"s_raw{i}") for i in range(2)]
        s_keys = sem("s_keys")
        s_ohjt = sem("s_ohjt")
        s_oh = sem("s_oh")
        s_ohused = sem("s_ohused")
        s_evict = sem("s_evict")
        s_w = sem("s_w")
        s_x = sem("s_x")
        s_xpad = sem("s_xpad")
        s_cst = sem("s_cst")
        s_t7 = sem("s_t7")
        s_t7r = sem("s_t7r")
        s_dmax = sem("s_dmax")
        s_dsq = sem("s_dsq")
        s_nrm = sem("s_nrm")
        s_gh = sem("s_gh")
        s_agg = sem("s_agg")
        s_plo = sem("s_plo")
        s_free = sem("s_free")
        s_xc = sem("s_xc")
        s_xcu = sem("s_xcu")
        s_var = sem("s_var")
        s_sd = sem("s_sd")
        s_o = sem("s_o")
        s_m7 = sem("s_m7")
        s_oT = sem("s_oT")
        s_h = sem("s_h")
        s_hT = sem("s_hT")
        s_bnv = sem("s_bnv")
        s_bnsd = sem("s_bnsd")
        s_bn = sem("s_bn")
        s_row1 = sem("s_row1")
        s_relu = sem("s_relu")
        s_y = sem("s_y")
        s_x3 = sem("s_x3")
        s_asad = sem("s_asad")
        s_selfl = sem("s_selfl")
        s_am = sem("s_am")
        s_A = sem("s_A")
        s_arg = sem("s_arg")
        s_exp = sem("s_exp")
        s_heads = sem("s_heads")
        s_hd = sem("s_hd")
        s_xw = sem("s_xw")
        s_xwu = sem("s_xwu")
        s_vg = sem("s_vg")
        s_vhi = sem("s_vhi")
        s_vd = sem("s_vd")
        s_F = sem("s_F")
        s_S = sem("s_S")
        s_post = sem("s_post")
        s_nad = sem("s_nad")
        s_M = sem("s_M")
        s_Mu = sem("s_Mu")
        s_c2 = sem("s_c2")
        s_ring = sem("s_ring")
        s_fin = sem("s_fin")
        s_eaev = sem("s_eaev")
        s_degacc = sem("s_degacc")
        s_hi = sem("s_hi")
        s_dif = sem("s_dif")
        s_lo = sem("s_lo")
        s_v = sem("s_v")
        s_g = sem("s_g")
        s_out = sem("s_out")

        block = ctx.enter_context(nc.Block())

        @block.sync
        def _(sp):
            sp.dma_start(fs[0:1, 0:R].bitcast(I32), dst.rearrange("(r c) -> c r", c=ROW)[0:1, :], allow_slow_non_contiguous=True).then_inc(s_first, 16)
            sp.wait_ge(s_start, 1)
            sp.dma_start(starts_d.ap().rearrange("(p b) -> p b", b=2), st_i[:]).then_inc(s_startd, 16)
            sp.wait_ge(s_startd, 16)
            sp.dma_start(starts_row[:], starts_d.ap()[None, :]).then_inc(s_startrow, 16)
            sp.wait_ge(s_startrow, 16)

            def load_group(g, par):
                for w in range(WG):
                    s = sp.value_load(starts_row[0:1, bass.ds(g * WG + w, 1)], min_val=0, max_val=E - SLOT)
                    sp.dma_start(raw[:, par, w, :], edges[bass.ds(s, SLOT), :].rearrange("(p k) c -> p (k c)", k=K)).then_inc(s_raw[par], 16)
            for g in range(2):
                load_group(g, g)
            with sp.Fori(0, G // 2 - 1) as i:
                for par in range(2):
                    g = i * 2 + (2 + par)
                    sp.wait_ge(s_lo, g - 1)
                    sp.wait_ge(s_keys, g - 1)
                    load_group(g, par)
            sp.wait_ge(s_degacc, 1)
            sp.wait_ge(s_lo, G)
            sp.wait_ge(s_xpad, 1)
            sp.dma_start(xs[:, 0:T - 1, :], x[0:(T - 1) * P, :].rearrange("(t p) d -> p t d", p=P)).then_inc(s_x, 16)
            sp.dma_start(xs[0:LAST, T - 1, :], x[(T - 1) * P:N, :]).then_inc(s_x, 16)
            for e, a_ in enumerate((att_s, att_d)):
                sp.dma_start(att[:, e], a_.to_broadcast([D, H, D])).then_inc(s_x, 16)
            for b, (t0, n) in enumerate(BL):
                sp.wait_ge(s_fin, b + 1)
                if t0 + n == T:
                    if n > 1:
                        sp.dma_start(out[t0 * P:(T - 1) * P, :].rearrange("(t p) d -> p t d", p=P), acc[:, t0:T - 1, :]).then_inc(s_out, 16)
                    sp.dma_start(out[(T - 1) * P:N, :], acc[0:LAST, T - 1, :]).then_inc(s_out, 16)
                else:
                    sp.dma_start(out[t0 * P:(t0 + n) * P, :].rearrange("(t p) d -> p t d", p=P), acc[:, t0:t0 + n, :]).then_inc(s_out, 16)
            sp.wait_ge(s_out, 16 * NB)

        @block.gpsimd
        def _(pool):
            pool.memset(ones[:], 1.0).then_inc(s_ones, 1)
            pool.memset(ident[:], 0.0).then_inc(s_g, 1)
            pool.memset(row64[:], 0.0).then_inc(s_g, 1)
            pool.memset(eps_c[:], EPS).then_inc(s_cst, 1)
            pool.wait_ge(s_g, 2)
            pool.affine_select(out=ident[:], in_=ident[:], compare_op=ALU.not_equal, fill=1.0, base=0, pattern=[[-1, P]], channel_multiplier=1).then_inc(s_cst, 1)
            pool.wait_ge(s_cst, 2)
            pool.memset(row64[D:S1, :], 1.0).then_inc(s_cst, 1)
            pool.wait_ge(s_cst, 3)
            pool.tensor_copy(ident16[:], ident[:]).then_inc(s_cst, 1)
            pool.iota(wlo[:], pattern=[[W, 2]], base=0, channel_multiplier=2 * W, allow_small_or_imprecise_dtypes=True).then_inc(s_iota, 1)
            pool.iota(iota_p[:], pattern=[[1, P]], base=0, channel_multiplier=0, allow_small_or_imprecise_dtypes=True).then_inc(s_iota, 1)
            pool.iota(iota_key[:], pattern=[[1, T], [T, W]], base=0, channel_multiplier=0, allow_small_or_imprecise_dtypes=True).then_inc(s_iota, 1)
            pool.iota(iota_j[:], pattern=[[1, W], [0, NC]], base=0, channel_multiplier=0, allow_small_or_imprecise_dtypes=True).then_inc(s_iota, 1)
            pool.iota(iota_t[:], pattern=[[1, T], [0, NC]], base=1, channel_multiplier=0, allow_small_or_imprecise_dtypes=True).then_inc(s_iota, 1)
            pool.iota(woff[:], pattern=[[W, WG], [0, K]], base=0, channel_multiplier=0, allow_small_or_imprecise_dtypes=True).then_inc(s_iota, 1)
            pool.wait_ge(s_rowidx, 1)
            for b in range(2):
                pool.indirect_dma_start(out=rows_i[:, b, :], out_offset=None, in_=dst.rearrange("(r c) -> r c", c=ROW),
                                        in_offset=bass.IndirectOffsetOnAxis(ap=row_i[:, b:b + 1], axis=0)).then_inc(s_rows, 16)
            pool.memset(C[:, :, NW:TP], 0.0).then_inc(s_iota, 1)
            pool.memset(eaT[:, NW:TP], 0.0).then_inc(s_iota, 1)
            pool.memset(eahl[:, :, 2 * DE:2 * DE + 1], 1.0).then_inc(s_iota, 1)
            pool.wait_ge(s_iota, 9)
            with pool.Fori(0, G // 2) as i:
                for par in range(2):
                    g = i * 2 + par
                    pool.wait_ge(s_hi, g + 1)
                    ea = raw[:, par].bitcast(F32).rearrange("p w (k c) -> p (w k) c", k=K)[:, :, 2:]
                    pool.tensor_tensor(ea, ea, eahl[:, :, 0:DE], ALU.subtract).then_inc(s_dif, 1)

            pool.wait_ge(s_degacc, 1)
            pool.wait_ge(s_lo, G)
            pool.memset(xs[:, T - 1, :], 0.0).then_inc(s_xpad, 1)
            pool.wait_ge(s_nrm, 1)
            pool.wait_ge(s_x, 64)

            def side(kk, b):
                t0, n = BL[b]
                m = kk * NB + b
                pool.wait_ge(s_xcu, m + (1 + (b == 0)))
                pool.tensor_tensor(xc[:, b % 2, 0:n, :], xs[:, t0:t0 + n, :], nrm[:, 3, t0:t0 + n, None].to_broadcast([P, n, D]), ALU.mult).then_inc(s_xc, 1)
            with pool.Fori(0, 4) as i:
                for par in range(2):
                    for b in range(NB):
                        side(i * 2 + par, b)
            for b in range(NB):
                side(8, b)
            pool.wait_ge(s_m7, NB)
            pool.wait_ge(s_xc, 9 * NB)
            pool.memset(eaT[D:S1, :], 1.0).then_inc(s_row1, 1)
            pool.wait_ge(s_row1, 1)
            for b, (t0, n) in enumerate(BL):
                m = 9 * NB + b
                pool.wait_ge(s_free, 12 * NB + b + 1)
                if b >= 2:
                    pool.wait_ge(s_y, NB + b - 1)
                    pool.wait_ge(s_xcu, m + 1)
                pool.tensor_copy(z[:, b % 2, 0:n, D:2 * D], xs[:, t0:t0 + n, :]).then_inc(s_g, 1)
                pool.tensor_tensor(xc[:, b % 2, 0:n, :], xs[:, t0:t0 + n, :], biases[:, 0:1, :].to_broadcast([P, n, D]), ALU.add).then_inc(s_g, 1)
                pool.wait_ge(s_g, 2 + 3 * b + 2)
                pool.tensor_tensor(xc[:, b % 2, 0:n, :], xc[:, b % 2, 0:n, :], biases[:, 1:2, :].to_broadcast([P, n, D]), ALU.add).then_inc(s_g, 1)
                pool.wait_ge(s_g, 2 + 3 * b + 3)
                pool.sem_inc(s_xc, 1)
            pool.wait_ge(s_am, 1)
            pool.partition_all_reduce(amax[:, 1, :], amax[:, 0, :], P, bass.bass_isa.ReduceOp.max).then_inc(s_A, 1)
            pool.wait_ge(s_heads, 1)
            with pool.Fori(0, H) as h:
                pool.wait_ge(s_post, h * NB + 1)
                pool.tensor_copy(hd[:], heads[:, bass.ds(h, 1), :, :].rearrange("p o a t -> p (o a) t")).then_inc(s_hd, 1)
                pool.tensor_copy(wgh[:], wg[:, bass.ds(h, 1), :].rearrange("p o d -> p (o d)")).then_inc(s_hd, 1)
                pool.tensor_copy(wadb[:], nwa[:, bass.ds(h, 1)].to_broadcast([D, P])).then_inc(s_hd, 1)
                for b, (t0, n) in enumerate(BL):
                    for e in range(2):
                        m = h * (2 * NB) + (2 * b + e)
                        pool.wait_ge(s_vhi, m + 1)
                        o = 2 * S1 * e
                        pool.tensor_tensor(Vd[:, e, 0:n, :], Vg[:, e, 0:n, :], F[:, t0:t0 + n, o:o + S1], ALU.subtract).then_inc(s_vd, 1)

        @block.scalar
        def _(act):
            act.sem_inc(s_evict, 2)
            for o_, i_ in ((weS[0:DE, :], We), (weS[DE:2 * DE, :], We), (weS[2 * DE:S1, :], be[None, :]), (w1[:], W1), (w2[0:D, :], W2),
                           (w2[D:S1, :], b2[None, :]), (wlr[:, 0:D], Wl), (wlr[:, D:2 * D], Wr), (wg[:], Wg.rearrange("k (h d) -> k h d", h=H)),
                           (biases[:, 0], bl[None, :].to_broadcast([P, D])), (biases[:, 1], br[None, :].to_broadcast([P, D])),
                           (biases[:, 2], bias_g[None, :].to_broadcast([P, D]))):
                act.dma_start(o_, i_).then_inc(s_w, 16)
            for j_, i_ in enumerate((b1, gamma, beta)):
                act.dma_start(vecs[:, j_:j_ + 1], i_[:, None]).then_inc(s_w, 16)
            WL = 15 * 16
            act.wait_ge(s_iota, 9)

            def lo_hi(i, par):
                g = i * 2 + par
                ea = raw[:, par].bitcast(F32).rearrange("p w (k c) -> p (w k) c", k=K)[:, :, 2:]
                act.wait_ge(s_raw[par], i * (16 * WG) + 16 * WG)
                act.activation(eahl[:, :, 0:DE], ea, ACT.Copy).then_inc(s_hi, 1)
                act.wait_ge(s_dif, g + 1)
                act.activation(eahl[:, :, DE:2 * DE], ea, ACT.Copy, scale=LO).then_inc(s_lo, 1)

            def evict(i, par):
                g = i * 2 + par
                for w in range(WG):
                    wi = g * WG + w
                    act.wait_ge(s_ohused, wi + 3)
                    act.activation(C[:, :, bass.ds(wi * W, W)], pk[(par * WG + w) % 2][:, 0:KEY].rearrange("p (t j) -> p t j", j=W), ACT.Copy).then_inc(s_evict, 1)
                act.wait_ge(s_ohused, (g + 1) * WG + 2)
                act.activation(eaT[:, bass.ds(g * (WG * W), WG * W)], pea[par][0:65, 0:WG * W], ACT.Copy).then_inc(s_eaev, 1)

            with act.Fori(0, G // 2) as i:
                for par in range(2):
                    g = i * 2 + par
                    act.wait_ge(s_ohused, g * WG + 2)
                    lo_hi(i, par)
                    evict(i, par)

            def low(kk, b, extra=0):
                t0, n = BL[b]
                act.wait_ge(s_agg, kk * NB + (b + 1))
                if isinstance(kk, int) and kk >= 10:
                    if b >= 2 and kk != 11:
                        act.wait_ge(s_o, (kk - 10) // 2 * NB + b - 1)
                    elif kk == 11 and b < 2:
                        act.wait_ge(s_o, NB)
                    else:
                        act.wait_ge(s_free, kk * NB + NB + b - 1 + (b == 0))
                else:
                    act.wait_ge(s_free, kk * NB + (NB + b - 1 + (b == 0)))
                act.activation(plo[:, b % 2, 0:n, :], bank[:, b, 0:n * 2 * D].rearrange("p (t c) -> p t c", c=2 * D)[:, :, D:2 * D], ACT.Copy, scale=1.0 / LO).then_inc(s_plo, 1)

            def root(m, n):
                act.wait_ge(s_var, m + 1)
                act.activation(sd[:, 0:n], mv[:, 0:n, 1], ACT.Sqrt, bias=eps_c[:]).then_inc(s_sd, 1)

            act.wait_ge(s_dmax, 1)
            act.activation(nrm[:, 0:2, :], nrm[:, 2:4, :], ACT.Sqrt).then_inc(s_dsq, 1)
            with act.Fori(0, 4) as i:
                for par in range(2):
                    for b in range(NB):
                        low(i * 2 + par, b)
            for b in range(NB):
                low(8, b)
            for b in range(NB):
                low(9, b)
                root(b, BL[b][1])
            def l1_take(b):
                t0, n = BL[b]
                act.wait_ge(s_m7, b + 1)
                act.activation(zT[0:D, b % 2, 0:n * P], bank[0:D, 7, 0:n * P], ACT.Copy).then_inc(s_oT, 1)

            def l1_take2(b):
                t0, n = BL[b]
                act.wait_ge(s_h, b + 1)
                act.activation(eaT[0:D, t0 * P:(t0 + n) * P], bank[0:D, b, 0:n * P], ACT.Identity, bias=vecs[:, 0:1]).then_inc(s_hT, 1)
            for b in range(NB + 2):
                if b < NB:
                    low(10, b)
                if 1 <= b <= NB:
                    l1_take(b - 1)
                if b >= 2:
                    l1_take2(b - 2)
            act.wait_ge(s_bnv, 1)
            act.activation(bnv[:, 2:3], bnv[:, 1:2], ACT.Sqrt, bias=eps_c[0:D, :]).then_inc(s_bnsd, 1)
            act.wait_ge(s_bn, 1)
            for b, (t0, n) in enumerate(BL):
                act.activation(eaT[0:D, t0 * P:(t0 + n) * P], eaT[0:D, t0 * P:(t0 + n) * P], ACT.Relu, bias=bnv[:, 5:6], scale=bnv[:, 4:5]).then_inc(s_relu, 1)
                if b >= 1:
                    root(NB + b - 1, BL[b - 1][1])
            root(2 * NB - 1, BL[-1][1])
            for b in range(NB):
                low(11, b)

            def l2_take(b):
                n = BL[b][1]
                act.wait_ge(s_m7, NB + b + 1)
                act.activation(zT[:, b % 2, 0:n * P], bank[:, 7, 0:n * P], ACT.Copy).then_inc(s_oT, 1)
            for b in range(NB + 2):
                if b < NB:
                    low(12, b)
                if 1 <= b <= NB:
                    l2_take(b - 1)
                if b >= 2:
                    root(2 * NB + b - 2, BL[b - 2][1])
            for b, (t0, n) in enumerate(BL):
                act.wait_ge(s_m7, 2 * NB + b + 1)
                act.activation(eaT[0:D, t0 * P:(t0 + n) * P], bank[0:D, 7, 0:n * P], ACT.Copy).then_inc(s_oT, 1)
            act.wait_ge(s_arg, 1)
            act.activation(heads[:, :, 1:5, :], heads[:, :, 1:5, :], ACT.Exp).then_inc(s_exp, 1)
            with act.Fori(0, H) as h:
                for b, (t0, n) in enumerate(BL):
                    for e in range(2):
                        m = h * (2 * NB) + (2 * b + e)
                        o = 2 * S1 * e
                        act.wait_ge(s_vg, m + 1)
                        act.wait_ge(s_ring, h * T + 1)
                        act.activation(F[:, t0:t0 + n, o:o + S1], Vg[:, e, 0:n, :], ACT.Copy).then_inc(s_vhi, 1)
                    for e in range(2):
                        m = h * (2 * NB) + (2 * b + e)
                        o = 2 * S1 * e
                        act.wait_ge(s_vd, m + 1)
                        act.activation(F[:, t0:t0 + n, o + S1:o + 2 * S1], Vd[:, e, 0:n, :], ACT.Copy, scale=LO).then_inc(s_F, 1)
                for b, (t0, n) in enumerate(BL):
                    act.wait_ge(s_Mu, h * (NB * T) + ((b + 1) * T + RB))
                    for jj in range(n):
                        t = t0 + jj
                        act.wait_ge(s_post, h * NB + (b + 1))
                        act.activation(r1[:, jj], bank[:, t % RB, 0:2 * S1], ACT.Identity, scale=hd[:, 3, t:t + 1]).then_inc(s_c2, 1)
                        act.activation(c2[:, jj], bank[:, t % RB, 4 * S1:6 * S1], ACT.Copy).then_inc(s_c2, 1)
            for b, (t0, n) in enumerate(BL):
                root(3 * NB + b, n)

        @block.vector
        def _(v):
            c = Count(v, s_v)
            v.wait_ge(s_first, 16)
            c.add(v.tensor_copy(first_f, fs[0:1, 0:R].bitcast(I32)))
            c.here()
            v.tensor_scalar(first_f, first_f, 0.0, None, ALU.add).then_inc(s_firstf, 1)
            v.wait_ge(s_firstb, 1)
            v.wait_ge(s_iota, 6)
            c.add(v.tensor_copy(fb[:], pf[:, 0:R]))
            c.here()
            for b in range(2):
                c.add(v.tensor_scalar(fs[:], fb[:], wlo[:, b:b + 1], None, ALU.is_lt, ALU.add, accum_out=cnt[:, b:b + 1]))
                c.here()
            c.add(v.tensor_scalar(cnt[:, 2:4], cnt[:, 0:2], -1.0, 0.0, ALU.add, ALU.max))
            c.here()
            v.tensor_copy(row_i[:], cnt[:, 2:4]).then_inc(s_rowidx, 1)
            v.wait_ge(s_rows, 32)
            for b in range(2):
                c.add(v.tensor_copy(fb[:, b * ROW:(b + 1) * ROW], rows_i[:, b]))
                c.here()
                c.add(v.tensor_scalar(fs[:, 0:ROW], fb[:, b * ROW:(b + 1) * ROW], wlo[:, b:b + 1], None, ALU.is_lt, ALU.add, accum_out=cnt[:, 4 + b:5 + b]))
                c.here()
            c.add(v.scalar_tensor_tensor(cnt[:, 6:8], cnt[:, 2:4], float(ROW), cnt[:, 4:6], ALU.mult, ALU.add))
            c.here()
            c.add(v.tensor_scalar(cnt[:, 0:2], cnt[:, 6:8], float(E - SLOT), None, ALU.min))
            c.here()
            v.tensor_copy(st_i[:], cnt[:, 0:2]).then_inc(s_start, 1)
            c.add(v.memset(dego[:], 0.0))
            with v.Fori(0, G // 2) as i:
                per = 2 * 12
                c.loop(i, per)
                for par in range(2):
                    g = i * 2 + par
                    v.wait_ge(s_raw[par], i * (16 * WG) + 16 * WG)
                    srci = raw[:, par].rearrange("p w (k c) -> p w k c", k=K)[:, :, :, 0]
                    dsti = raw[:, par].rearrange("p w (k c) -> p w k c", k=K)[:, :, :, 1]
                    c.here()
                    c.add(v.tensor_scalar(ki[:, 0], srci, 7, None, ALU.arith_shift_right))
                    c.add(v.tensor_scalar(ki[:, 1], srci, 127, None, ALU.bitwise_and))
                    c.add(v.tensor_tensor(kf[:, 0], dsti, woff[:], ALU.subtract))
                    c.here()
                    c.add(v.tensor_copy(kf[:, 1], ki[:, 0]))
                    c.add(v.tensor_copy(kf[:, 2], ki[:, 1]))
                    c.add(v.tensor_scalar(woff[:], woff[:], float(W * WG), None, ALU.add))
                    c.add(v.tensor_copy(dl16[:, par], kf[:, 0]))
                    c.here()
                    c.add(v.scalar_tensor_tensor(kf[:, 3], kf[:, 0], float(T), kf[:, 1], ALU.mult, ALU.add))
                    c.add(v.tensor_tensor(ohj[:, par], iota_j[:], dl16[:, par].rearrange("p w k -> p (w k)")[:, None, :].to_broadcast([P, W, NC]), ALU.is_equal))
                    c.here()
                    c.add(v.tensor_reduce(kf[:, 4].rearrange("p w k -> p (w k)"), ohj[:, par].rearrange("p j c -> p c j"), AX, ALU.add))
                    c.here()
                    c.add(v.scalar_tensor_tensor(tv16[:], kf[:, 1], 1.0, kf[:, 4], ALU.add, ALU.mult))
                    c.here()
                    v.tensor_tensor(oht[:, par], iota_t[:], tv16[:].rearrange("p w k -> p (w k)")[:, None, :].to_broadcast([P, T, NC]), ALU.is_equal).then_inc(s_keys, 1)
                    for w in range(WG):
                        wi = g * WG + w
                        r = (par * WG + w) % 2
                        v.wait_ge(s_ohused, wi + 1)
                        for k in range(K):
                            v.tensor_scalar(ohp[:, r, k], iota_p[:], kf[:, 2, w, k:k + 1], None, ALU.is_equal)
                            last = v.tensor_scalar(ohk[:, r, k], iota_key[:].rearrange("p t j -> p (t j)"), kf[:, 3, w, k:k + 1], None, ALU.is_equal)
                        last.then_inc(s_oh, 1)
                    v.wait_ge(s_ohused, (g + 1) * WG + 2)
                    c.add(v.tensor_tensor(dego[:], pdeg[par][:, 0:T], dego[:], ALU.add))
                c.end(G // 2)
            c.here()
            v.tensor_copy(kf[:, 4, 0, 0:1], kf[:, 3, 0, 0:1]).then_inc(s_degacc, 1)
            v.sem_inc(s_free, NB)
            WL = 15 * 16
            v.wait_ge(s_w, WL)
            v.wait_ge(s_x, 64)
            c.add(v.tensor_scalar(weS[DE:2 * DE, :], weS[DE:2 * DE, :], 1.0 / LO, None, ALU.mult))
            for e in range(2):
                c.add(v.tensor_tensor(att[:, e], att[:, e], wg[:], ALU.mult))
            c.here()
            v.tensor_reduce(wa[:], att[:], AX, ALU.add).then_inc(s_t7r, 1)
            v.wait_ge(s_t7r, 1)
            c.add(v.tensor_scalar(nwa[:], wa[:, 1, :], -1.0, None, ALU.mult))
            v.wait_ge(s_t7, 1)
            c.add(v.tensor_scalar(nrm[:, 3, :], bank[:, 7, 0:T], 1.0, None, ALU.max))
            c.add(v.tensor_copy(wlrT[:], bank[:, 7, P:P + D]))
            c.here()
            v.tensor_scalar(nrm[:, 2, :], dego[:], 1.0, None, ALU.max).then_inc(s_dmax, 1)
            v.wait_ge(s_dsq, 1)
            c.add(v.reciprocal(nrm[:, 4:6, :], nrm[:, 0:2, :]))
            c.here()
            ns, nd = nrm[:, 4, :], nrm[:, 5, :]
            c.add(v.tensor_tensor(nrm[:, 6, :], ns, nd, ALU.mult))
            c.add(v.tensor_scalar(nrm[:, 7, :], ns, LO, None, ALU.mult))
            c.add(v.tensor_scalar(nrm[:, 8, :], nd, 0.9, None, ALU.mult))
            c.add(v.tensor_scalar(nrm[:, 9, :], nd, LO, None, ALU.mult))
            c.here()
            c.add(v.tensor_scalar(nrm[:, 2, :], nrm[:, 6, :], 0.9 * LO, None, ALU.mult))
            c.add(v.tensor_tensor(nrm[:, 10, :], nrm[:, 9, :], nd, ALU.mult))
            v.tensor_scalar(nrm[:, 3, :], ns, 0.1 * LO, None, ALU.mult).then_inc(s_nrm, 1)
            v.wait_ge(s_nrm, 1)

            def cols(row, t0, n):
                return nrm[:, row, t0:t0 + n, None].to_broadcast([P, n, D])

            def split(src, par, t0, n):
                c.here()
                c.add(v.tensor_scalar(GH[:, par, t0:t0 + n, 0:D], src, 1.0 / LO, None, ALU.mult))
                c.here()
                v.scalar_tensor_tensor(GH[:, par, t0:t0 + n, D:2 * D], GH[:, par, t0:t0 + n, 0:D], -LO, src, ALU.mult, ALU.add).then_inc(s_gh, 1)

            v.wait_ge(s_x, 64)
            for b, (t0, n) in enumerate(BL):
                if b >= 2:
                    v.wait_ge(s_gh, b - 1)
                c.add(v.tensor_tensor(V[:, b % 2, 0:n, :], xs[:, t0:t0 + n, :], cols(7, t0, n), ALU.mult))
                split(V[:, b % 2, 0:n, :], 0, t0, n)

            def high(b, n):
                return bank[:, b, 0:n * 2 * D].rearrange("p (t c) -> p t c", c=2 * D)[:, :, 0:D]

            def sums(kk, b, frees):
                t0, n = BL[b]
                v.wait_ge(s_plo, kk * NB + (b + 1))
                c.here()
                ins = v.tensor_tensor(S[:, b % 2, 0:n, :], high(b, n), plo[:, b % 2, 0:n, :], ALU.add)
                if frees:
                    ins.then_inc(s_free, 1)
                    v.wait_ge(s_free, kk * NB + (NB + b + 1))
                else:
                    c.add(ins)
                    c.here()
                return S[:, b % 2, 0:n, :]

            def l0_block(kk, b, par):
                t0, n = BL[b]
                s_ = sums(kk, b, True)
                c.add(v.tensor_tensor(s_, s_, cols(2, t0, n), ALU.mult))
                c.here()
                v.wait_ge(s_xc, kk * NB + (b + 1))
                v.wait_ge(s_gh, kk * NB + (NB + b - 1 + (b == 0)))
                v.tensor_tensor(V[:, b % 2, 0:n, :], s_, xc[:, b % 2, 0:n, :], ALU.add).then_inc(s_xcu, 1)
                v.wait_ge(s_xcu, kk * NB + (b + 3))
                split(V[:, b % 2, 0:n, :], par, t0, n)

            v.sem_inc(s_xcu, 2)
            with v.Fori(0, 4) as i:
                c.loop(i, 2 * NB * 2)
                for par in range(2):
                    for b in range(NB):
                        l0_block(i * 2 + par, b, 1 - par)
                c.end(4)
            for b in range(NB):
                l0_block(8, b, 1)

            def norm(m, y, n, o):
                c.here()
                for j in range(n):
                    c.add(v.bn_stats(small[:, 6 * j:6 * j + 6], y[:, j, :]))
                c.here()
                for j in range(n):
                    last = v.bn_aggr(mv[:, j, :], small[:, 6 * j:6 * j + 6])
                    if j < n - 1:
                        c.add(last)
                last.then_inc(s_var, 1)
                v.wait_ge(s_var, m + 1)
                v.wait_ge(s_sd, m + 1)
                c.add(v.reciprocal(small[:, 32:32 + n], sd[:, 0:n]))
                c.here()
                for j in range(n):
                    last = v.tensor_scalar(o[:, j, :], y[:, j, :], mv[:, j, 0:1], small[:, 32 + j:33 + j], ALU.subtract, ALU.mult)
                    if j < n - 1:
                        c.add(last)
                return last

            for b, (t0, n) in enumerate(BL):
                s_ = sums(9, b, True)
                xb = xs[:, t0:t0 + n, :]
                c.add(v.tensor_tensor(s_, s_, cols(8, t0, n), ALU.mult))
                c.here()
                c.add(v.scalar_tensor_tensor(V[:, b % 2, 0:n, :], xb, 1.1, s_, ALU.mult, ALU.add))
                c.add(norm(b, V[:, b % 2, 0:n, :], n, xb))
                c.here()
                c.add(v.tensor_scalar(V[:, b % 2, 0:n, :], xb, LO, None, ALU.mult))
                split(V[:, b % 2, 0:n, :], 0, t0, n)

            for b in range(NB + 2):
                if b < NB:
                    t0, n = BL[b]
                    s_ = sums(10, b, False)
                    if b >= 2:
                        v.wait_ge(s_m7, b - 1)
                    v.tensor_tensor(z[:, b % 2, 0:n, 0:D], s_, xs[:, t0:t0 + n, :], ALU.add).then_inc(s_o, 1)
                if b >= 2:
                    t0, n = BL[b - 2]
                    v.wait_ge(s_hT, b - 1)
                    last = v.bn_stats(bst[:, b - 2, :], eaT[0:D, t0 * P:min((t0 + n) * P, N)])
                    c.add(last)
            c.here()
            v.bn_aggr(bnv[:, 0:2], bst[:].rearrange("p b s -> p (b s)")).then_inc(s_bnv, 1)
            v.wait_ge(s_bnsd, 1)
            c.add(v.reciprocal(bnv[:, 3:4], bnv[:, 2:3]))
            c.here()
            c.add(v.tensor_tensor(bnv[:, 4:5], bnv[:, 3:4], vecs[:, 1:2], ALU.mult))
            c.here()
            c.add(v.tensor_tensor(bnv[:, 6:7], bnv[:, 0:1], bnv[:, 4:5], ALU.mult))
            c.here()
            v.tensor_tensor(bnv[:, 5:6], vecs[:, 2:3], bnv[:, 6:7], ALU.subtract).then_inc(s_bn, 1)
            for b, (t0, n) in enumerate(BL):
                xb = xs[:, t0:t0 + n, :]
                v.wait_ge(s_y, b + 1)
                v.wait_ge(s_gh, 10 * NB + NB + b - 1 + (b == 0))
                v.tensor_tensor(V[:, b % 2, 0:n, :], bank[:, b, 0:n * D].rearrange("p (t d) -> p t d", d=D), xb, ALU.add).then_inc(s_free, 1)
                v.wait_ge(s_free, NB + 10 * NB + b + 1)
                c.add(norm(NB + b, V[:, b % 2, 0:n, :], n, xb))
                c.here()
                c.add(v.tensor_tensor(V[:, b % 2, 0:n, :], xb, cols(9, t0, n), ALU.mult))
                split(V[:, b % 2, 0:n, :], 1, t0, n)
            for b, (t0, n) in enumerate(BL):
                s_ = sums(11, b, True)
                v.wait_ge(s_gh, 11 * NB + NB + b - 1 + (b == 0))
                c.add(v.tensor_tensor(V[:, b % 2, 0:n, :], s_, cols(10, t0, n), ALU.mult))
                split(V[:, b % 2, 0:n, :], 0, t0, n)
            for b in range(NB + 2):
                if b < NB:
                    t0, n = BL[b]
                    s_ = sums(12, b, False)
                    if b >= 2:
                        v.wait_ge(s_m7, NB + b - 1)
                    v.tensor_tensor(z[:, b % 2, 0:n, 0:D], s_, cols(5, t0, n), ALU.mult).then_inc(s_o, 1)
                if b >= 2:
                    t0, n = BL[b - 2]
                    v.wait_ge(s_y, NB + b - 1)
                    v.wait_ge(s_xc, 9 * NB + b - 1)
                    v.tensor_tensor(V[:, b % 2, 0:n, :], bank[:, b - 2, 0:n * D].rearrange("p (t d) -> p t d", d=D), xc[:, b % 2, 0:n, :], ALU.add).then_inc(s_xcu, 1)
                    v.wait_ge(s_xcu, 9 * NB + b - 1 + 2)
                    norm(2 * NB + b - 2, V[:, b % 2, 0:n, :], n, xs[:, t0:t0 + n, :]).then_inc(s_x3, 1)
            v.wait_ge(s_agg, 13 * NB)
            v.wait_ge(s_cst, 4)
            for t in range(T):
                v.tensor_tensor(C[:, t, t * P:(t + 1) * P], C[:, t, t * P:(t + 1) * P], ident16[:], ALU.add).then_inc(s_selfl, 1)
            for b, (t0, n) in enumerate(BL):
                v.wait_ge(s_asad, b + 1)
                c.add(v.tensor_copy(asad[:, :, :, t0:t0 + n].rearrange("p e h t -> p (e h) t"), bank[:, b, 0:n * 2 * H].rearrange("p (t e) -> p e t", e=2 * H)))
            c.here()
            v.tensor_reduce(amax[:, 0, :], asad[:, 0], AX, ALU.max).then_inc(s_am, 1)
            v.wait_ge(s_A, 1)
            Ab = amax[:, 1, :, None].to_broadcast([P, H, T])
            c.add(v.tensor_copy(heads[:, :, 0, :], asad[:, 0]))
            c.add(v.tensor_tensor(heads[:, :, 1, :], asad[:, 0], Ab, ALU.subtract))
            c.add(v.tensor_tensor(heads[:, :, 4, :], asad[:, 1], Ab, ALU.add))
            c.here()
            c.add(v.tensor_scalar(heads[:, :, 2, :], heads[:, :, 1, :], 0.2, None, ALU.mult))
            c.add(v.tensor_scalar(heads[:, :, 3, :], heads[:, :, 4, :], 0.2, None, ALU.mult))
            c.here()
            c.add(v.tensor_tensor(asad[:, 1], heads[:, :, 4, :], heads[:, :, 3, :], ALU.max))
            c.here()
            c.add(v.tensor_tensor(asad[:, 0], heads[:, :, 3, :], asad[:, 1], ALU.subtract))
            c.here()
            c.add(v.tensor_tensor(heads[:, :, 3, :], heads[:, :, 4, :], asad[:, 1], ALU.subtract))
            c.here()
            v.tensor_copy(heads[:, :, 4, :], asad[:, 0]).then_inc(s_arg, 1)
            v.wait_ge(s_exp, 1)
            c.add(v.memset(acc[:], 0.0))
            v.tensor_scalar(heads[:, :, 1:3, :], heads[:, :, 1:3, :], XS, None, ALU.mult).then_inc(s_heads, 1)
            v.wait_ge(s_selfl, T)
            v.sem_inc(s_ring, 1)
            v.sem_inc(s_post, 1)
            with v.Fori(0, H) as h:
                c.loop(h, NB + 2 * T + 3 * NB - NB)
                v.wait_ge(s_hd, h * 3 + 3)
                for b, (t0, n) in enumerate(BL):
                    v.wait_ge(s_xw, h * NB + (b + 1))
                    for e in range(2):
                        if b >= 1:
                            v.wait_ge(s_vd, h * (2 * NB) + (2 * (b - 1) + e + 1))
                            v.wait_ge(s_vhi, h * (2 * NB) + (2 * (b - 1) + e + 1))
                        last = v.tensor_tensor(Vg[:, e, 0:n, 0:D], bank[:, 7, 0:n * D].rearrange("p (t d) -> p t d", d=D), hd[:, 1 + e, t0:t0 + n, None].to_broadcast([P, n, D]), ALU.mult)
                        if e == 0:
                            c.add(last)
                        else:
                            last.then_inc(s_xwu, 1)
                        v.tensor_copy(Vg[:, e, 0:n, D:S1], hd[:, 1 + e, t0:t0 + n, None]).then_inc(s_vg, 1)
                    c.here()

                def post(b):
                    t0, n = BL[b]
                    for jj in range(n):
                        t = t0 + jj
                        v.wait_ge(s_c2, h * (2 * T) + (2 * t + 2))
                        v.tensor_tensor(c2[:, jj], c2[:, jj], bank[:, t % RB, 2 * S1:4 * S1], ALU.subtract).then_inc(s_ring, 1)
                        v.wait_ge(s_ring, h * T + (t + 2))
                        c.add(v.scalar_tensor_tensor(r1[:, jj], c2[:, jj], hd[:, 4, t:t + 1], r1[:, jj], ALU.mult, ALU.add))
                    c.here()
                    c.add(v.scalar_tensor_tensor(q[:, 0:n, :], r1[:, 0:n, S1:2 * S1], 1.0 / LO, r1[:, 0:n, 0:S1], ALU.mult, ALU.add))
                    c.here()
                    c.add(v.tensor_scalar(rd[:, 0:n], q[:, 0:n, D], 1e-16 * XS, float(H), ALU.add, ALU.mult))
                    c.here()
                    c.add(v.reciprocal(rd[:, 0:n], rd[:, 0:n]))
                    c.here()
                    for jj in range(n):
                        last = v.scalar_tensor_tensor(acc[:, t0 + jj, :], q[:, jj, 0:D], rd[:, jj:jj + 1], acc[:, t0 + jj, :], ALU.mult, ALU.add)
                        if jj < n - 1:
                            c.add(last)
                    last.then_inc(s_post, 1)

                for b, (t0, n) in enumerate(BL):
                    v.wait_ge(s_nad, h * NB + (b + 1))
                    for t in range(T):
                        mi = b * T + t
                        v.wait_ge(s_Mu, h * (NB * T) + (mi + 1))
                        v.scalar_tensor_tensor(Mr[:, mi % RB, 0:n * P], bank[:, 5 + b % 2, 0:n * P], hd[:, 0, t:t + 1], C[:, t, t0 * P:(t0 + n) * P], ALU.is_lt, ALU.mult).then_inc(s_M, 1)
                        if t == RB - 1 and b >= 1:
                            post(b - 1)
                post(NB - 1)
                c.end(H)
            v.wait_ge(s_post, H * NB + 1)
            for b, (t0, n) in enumerate(BL):
                c.here()
                c.add(v.tensor_tensor(acc[:, t0:t0 + n, :], acc[:, t0:t0 + n, :], xs[:, t0:t0 + n, :], ALU.add))
                c.here()
                c.add(v.tensor_tensor(acc[:, t0:t0 + n, :], acc[:, t0:t0 + n, :], biases[:, 2:3, :].to_broadcast([P, n, D]), ALU.add))
                norm(3 * NB + b, acc[:, t0:t0 + n, :], n, acc[:, t0:t0 + n, :]).then_inc(s_fin, 1)

        @block.tensor
        def _(pe):
            pe.sem_inc(s_ohused, 2)
            pe.wait_ge(s_firstf, 1)
            pe.wait_ge(s_ones, 1)
            pe.matmul(pf[:, 0:512], ones[:], first_f[:, 0:512], start=True, stop=True)
            pe.matmul(pf[:, 512:R], ones[:], first_f[:, 512:R], start=True, stop=True).then_inc(s_firstb, 1)
            with pe.Fori(0, G // 2) as i:
                for par in range(2):
                    g = i * 2 + par
                    pe.wait_ge(s_keys, g + 1)
                    pe.wait_ge(s_lo, g + 1)
                    for w in range(WG):
                        wi = g * WG + w
                        r = (par * WG + w) % 2
                        pe.wait_ge(s_oh, wi + 1)
                        pe.wait_ge(s_evict, wi + 1)
                        for k in range(K):
                            ch = w * K + k
                            pe.matmul(pk[r][:, 0:KEY], ohp[:, r, k], ohk[:, r, k], start=k == 0, stop=k == K - 1)
                            pe.matmul(pdeg[par][:, 0:T], ohp[:, r, k], oht[:, par, :, ch], start=ch == 0, stop=ch == NC - 1)
                            last = pe.matmul(pea[par][0:65, w * W:(w + 1) * W], eahl[:, ch, :], ohj[:, par, :, ch], start=k == 0, stop=k == K - 1)
                        last.then_inc(s_ohused, 1)

            WL = 15 * 16
            pe.wait_ge(s_w, WL)
            pe.wait_ge(s_eaev, G)
            pe.wait_ge(s_degacc, 1)
            pe.wait_ge(s_cst, 3)
            for t in range(T):
                pe.matmul(bank[:, 7, t:t + 1], eaT[:, t * P:(t + 1) * P], row64[:], start=t == 0, stop=False)
            pe.matmul(bank[:, 7, P:P + D], wlr[:], ident[0:D, 0:D], start=False, stop=True).then_inc(s_t7, 1)

            def hop(kk, par, after=None):
                for b, (t0, n) in enumerate(BL):
                    pe.wait_ge(s_free, kk * NB + (b + 1))
                    early = T - 5 if b == 0 else T
                    if b == 0:
                        pe.wait_ge(s_gh, kk * NB + (NB - 2))
                    for lo_, hi_ in ((0, early), (early, T)):
                        if lo_ == hi_:
                            continue
                        if lo_:
                            pe.wait_ge(s_gh, kk * NB + NB)
                        for jj in range(n):
                            for t in range(lo_, hi_):
                                last = pe.matmul(bank[:, b, jj * 2 * D:(jj + 1) * 2 * D], C[:, t, (t0 + jj) * P:(t0 + jj + 1) * P], GH[:, par, t, :],
                                                 start=t == 0 and jj == 0, stop=jj == n - 1 and t == T - 1)
                    last.then_inc(s_agg, 1)
                    if after:
                        after(b)

            with pe.Fori(0, 4) as i:
                for par in range(2):
                    hop(i * 2 + par, par)
            hop(8, 0)
            hop(9, 1)

            def l1_sum(b):
                t0, n = BL[b]
                pe.wait_ge(s_o, b + 1)
                if b >= 1:
                    pe.wait_ge(s_oT, b)
                pe.matmul(bank[0:D, 7, 0:n * P], weS[:], eaT[:, t0 * P:(t0 + n) * P], start=True, stop=False)
                for j in range(n):
                    last = pe.matmul(bank[0:D, 7, j * P:(j + 1) * P], z[:, b % 2, j, 0:D], ident[:], start=False, stop=j == n - 1)
                last.then_inc(s_m7, 1)

            def l1_up(b):
                t0, n = BL[b]
                pe.wait_ge(s_oT, b + 1)
                pe.matmul(bank[0:D, b, 0:n * P], w1[:], zT[0:D, b % 2, 0:n * P], start=True, stop=True).then_inc(s_h, 1)

            def after1(b):
                if b >= 1:
                    l1_sum(b - 1)
                if b >= 2:
                    l1_up(b - 2)
            hop(10, 0, after1)
            l1_sum(NB - 1)
            l1_up(NB - 2)
            l1_up(NB - 1)
            pe.wait_ge(s_row1, 1)
            for b, (t0, n) in enumerate(BL):
                pe.wait_ge(s_relu, b + 1)
                for j in range(n):
                    last = pe.matmul(bank[:, b, j * D:(j + 1) * D], eaT[:, (t0 + j) * P:(t0 + j + 1) * P], w2[:], start=j == 0, stop=j == n - 1)
                last.then_inc(s_y, 1)
            hop(11, 1)

            def l2_turn(b):
                n = BL[b][1]
                pe.wait_ge(s_o, NB + b + 1)
                pe.wait_ge(s_xc, 9 * NB + b + 1)
                pe.wait_ge(s_oT, NB + b)
                for j in range(n):
                    last = pe.matmul(bank[:, 7, j * P:(j + 1) * P], z[:, b % 2, j, :], ident[:], start=j == 0, stop=j == n - 1)
                last.then_inc(s_m7, 1)

            def l2_down(b):
                n = BL[b][1]
                pe.wait_ge(s_oT, NB + b + 1)
                for j in range(n):
                    last = pe.matmul(bank[:, b, j * D:(j + 1) * D], zT[:, b % 2, j * P:(j + 1) * P], wlrT[:], start=j == 0, stop=j == n - 1)
                last.then_inc(s_y, 1)

            def after2(b):
                if b >= 1:
                    l2_turn(b - 1)
                if b >= 2:
                    l2_down(b - 2)
            hop(12, 0, after2)
            l2_turn(NB - 1)
            l2_down(NB - 2)
            l2_down(NB - 1)
            pe.wait_ge(s_t7r, 1)
            for b in range(NB + 1):
                if b < NB:
                    t0, n = BL[b]
                    pe.wait_ge(s_x3, b + 1)
                    pe.wait_ge(s_oT, 2 * NB + b)
                    for j in range(n):
                        last = pe.matmul(bank[0:D, 7, j * P:(j + 1) * P], xs[:, t0 + j, :], ident[:], start=j == 0, stop=j == n - 1)
                    last.then_inc(s_m7, 1)
                if b >= 1:
                    t0, n = BL[b - 1]
                    pe.wait_ge(s_oT, 2 * NB + b)
                    for j in range(n):
                        last = pe.matmul(bank[:, b - 1, j * 2 * H:(j + 1) * 2 * H], eaT[0:D, (t0 + j) * P:(t0 + j + 1) * P], wa[:].rearrange("p e h -> p (e h)"), start=j == 0, stop=j == n - 1)
                    last.then_inc(s_asad, 1)
            pe.sem_inc(s_Mu, RB)
            with pe.Fori(0, H) as h:
                pe.wait_ge(s_hd, h * 3 + 3)
                pe.wait_ge(s_ring, h * T + 1)
                for b, (t0, n) in enumerate(BL):
                    if b >= 1:
                        pe.wait_ge(s_xwu, h * NB + b)
                    for j in range(n):
                        last = pe.matmul(bank[:, 7, j * D:(j + 1) * D], eaT[0:D, (t0 + j) * P:(t0 + j + 1) * P], wgh[:], start=j == 0, stop=j == n - 1)
                    last.then_inc(s_xw, 1)

                def nad(b):
                    t0, n = BL[b]
                    pe.matmul(bank[:, 5 + b % 2, 0:n * P], wadb[:], eaT[0:D, t0 * P:(t0 + n) * P], start=True, stop=True).then_inc(s_nad, 1)
                nad(0)
                nad(1)
                for b, (t0, n) in enumerate(BL):
                    for jj in range(n):
                        t_ = t0 + jj
                        if b == 0 and jj == 0:
                            pe.wait_ge(s_F, h * (2 * NB) + 2 * NB)
                        if t_ >= RB:
                            pe.wait_ge(s_ring, h * T + (t_ - RB + 2))
                        for t in range(T):
                            pe.matmul(bank[:, t_ % RB, 4 * S1:6 * S1], C[:, t, t_ * P:(t_ + 1) * P], F[:, t, 2 * S1:4 * S1], start=t == 0, stop=t == T - 1)
                    for t in range(T):
                        mi = b * T + t
                        pe.wait_ge(s_M, h * (NB * T) + (mi + 1))
                        for jj in range(n):
                            last = pe.matmul(bank[:, (t0 + jj) % RB, 0:4 * S1], Mr[:, mi % RB, jj * P:(jj + 1) * P], F[:, t, :], start=t == 0, stop=t == T - 1)
                        last.then_inc(s_Mu, 1)
                    if b + 2 < NB:
                        nad(b + 2)


_INS = ["L1_gnn_We", "L1_gnn_be", "L1_gnn_W1", "L1_gnn_b1", "L1_gnn_gamma", "L1_gnn_beta", "L1_gnn_W2", "L1_gnn_b2",
        "L2_gnn_W", "L2_gnn_b", "L2_gnn_Wr", "L2_gnn_br", "L3_gnn_W", "L3_gnn_att_src", "L3_gnn_att_dst", "L3_gnn_bias"]
_OUTS = [((3125, 64), "float32")]


def kernel(**inputs):
    import numpy as _np
    import concourse.bacc as _bacc
    from concourse import mybir as _mybir
    from concourse.bass_utils import run_bass_kernel_spmd as _run
    nc = _bacc.Bacc("TRN2", target_bir_lowering=False, num_devices=1, dynamic_dma_scratch_size=8192)
    arrays, args = {}, []
    packed = {k: _np.ascontiguousarray(inputs[k]) for k in ("x", "dst")}
    packed["edges"] = _np.concatenate([_np.asarray(inputs["src"])[:, None], _np.asarray(inputs["dst"])[:, None],
                                       _np.asarray(inputs["edge_attr_32"]).view(_np.int32)], axis=1)
    packed.update({k: _np.ascontiguousarray(inputs[k]) for k in _INS})
    for name, a in packed.items():
        arrays[f"in_{name}_dram"] = a
        args.append(nc.dram_tensor(f"in_{name}_dram", a.shape, _mybir.dt.from_np(a.dtype), kind="ExternalInput").ap())
    for i, (shape, dtype) in enumerate(_OUTS):
        dt = _mybir.dt.from_np(_np.dtype(dtype))
        args.append(nc.dram_tensor(f"out_{i}_dram", shape, dt, kind="ExternalOutput").ap())
    gnn_kernel(nc, *args)
    r = _run(nc, [arrays], core_ids=[0])
    got = tuple(r.results[0][f"out_{i}_dram"] for i in range(len(_OUTS)))
    return got[0]
```

```python
from contextlib import ExitStack
import concourse.bass as bass
from concourse import mybir

ALU = mybir.AluOpType
ACT = mybir.ActivationFunctionType
AX = mybir.AxisListType.X
F32 = mybir.dt.float32
F16 = mybir.dt.float16
BF16 = mybir.dt.bfloat16
I32 = mybir.dt.int32

P = 128
LO = 2048.0


class Count:

    def __init__(self, eng, sem):
        self.eng, self.sem, self.n, self.base = eng, sem, 0, 0

    def add(self, ins):
        ins.then_inc(self.sem, 1)
        self.n += 1
        return ins

    def here(self):
        self.eng.wait_ge(self.sem, self.base + self.n)

    def loop(self, i, per):
        self.base, self.n0, self.per = i * per, self.n, per

    def end(self, times):
        assert self.n - self.n0 == self.per, (self.n - self.n0, self.per)
        self.base, self.n = 0, self.n0 + self.per * times


def gnn_kernel(nc, x, dst, edges, We, be, W1, b1, gamma, beta, W2, b2, Wl, bl, Wr, br, Wg, att_s, att_d, bias_g, out):
    N, D = x.shape
    E = dst.shape[0]
    DE = edges.shape[1] - 2
    T = -(-N // P)
    W = 13
    K = 4
    WG = 11
    G = 22
    SLOT = P * K
    NW = W * WG * G
    ROW = 160
    R = E // ROW
    NC = WG * K
    KEY = T * W
    EC = K * (DE + 2)
    H = att_s.shape[1]
    TP = T * P
    BL = [(t, min(4, T - t)) for t in range(0, T, 4)]
    NB = len(BL)
    HOPS = 10
    EPS = 1e-5
    LAST = N - (T - 1) * P
    XS = 256.0
    S1 = D + 1
    RB = 5
    RING = 3
    KEEP = 2
    GE = 125
    GC = E // GE
    BIG = 3e38
    GS = H * D + H
    WIDEST = 16.0
    STEEP = 2.0 ** 40
    MOST = 2048.0

    with ExitStack() as ctx:
        def sb(name, shape, dt):
            return ctx.enter_context(nc.sbuf_tensor(name, shape, dt))

        def ps(name, shape, dt=F32):
            return ctx.enter_context(nc.psum_tensor(name, shape, dt))

        def sem(name):
            return ctx.enter_context(nc.semaphore(name))

        starts_d = nc.dram_tensor("starts_d", (256,), I32)
        C = sb("C", [P, T, TP], F16)
        eaT = sb("eaT", [65, TP], F32)
        starts_row = sb("starts_row", [1, 256], I32)
        dego = sb("dego", [P, T], F32)
        ones = sb("ones", [1, P], F32)
        first_f = eaT[0:1, 0:R]
        ident = sb("ident", [P, P], F32)
        ident16 = sb("ident16", [P, P], F16)
        row64 = sb("row64", [S1, 1], F32)
        eps_c = sb("eps_c", [P, 1], F32)
        wts = sb("wts", [P, 6 * D], F32)
        weS = wts[0:S1, 0:D]
        w1 = wts[0:D, D:2 * D]
        w2 = wts[0:S1, 2 * D:3 * D]
        vecs = sb("vecs", [D, 3], F32)
        wlr = wts[0:D, 3 * D:5 * D]
        wlrT = wts[:, 5 * D:6 * D]
        wg = sb("wg", [D, H, D], F32)
        wa = sb("wa", [D, 2, H], F32)
        nwa = sb("nwa", [D, H], F32)
        biases = sb("biases", [P, 3, D], F32)
        nrm = sb("nrm", [P, 12, T], F32)
        small = sb("small", [P, 64], F32)
        mv = sb("mv", [P, 4, 2], F32)
        onesP = sb("onesP", [P, 1], F32)
        chk = sb("chk", [P, 2], F32)
        chk1 = sb("chk1", [1, 8], F32)
        flag = sb("flag", [1, 2], I32)
        sd = sb("sd", [P, 4], F32)
        with ExitStack() as built:
            def bb(name, shape, dt):
                return built.enter_context(nc.sbuf_tensor(name, shape, dt))

            iota_p = bb("iota_p", [P, P, K], F16)
            iota_key = bb("iota_key", [P, T, W], F16)
            iota_j = bb("iota_j", [P, W, NC], F16)
            iota_t = bb("iota_t", [P, T, NC], F16)
            woff = bb("woff", [P, WG, K], F32)
            with ExitStack() as search:
                def tb(name, shape, dt):
                    return search.enter_context(nc.sbuf_tensor(name, shape, dt))

                fb = tb("fb", [P, R], F32)
                fs = tb("fs", [P, R], F32)
                wlo = tb("wlo", [P, 2], F32)
                cnt = tb("cnt", [P, 8], F32)
                row_i = tb("row_i", [P, 2], I32)
                rows_i = tb("rows_i", [P, 2, ROW], I32)
                st_i = tb("st_i", [P, 2], I32)
            raw = bb("raw", [P, 2, WG, EC], I32)
            ohp = bb("ohp", [P, RING, P, K], F16)
            ohk = bb("ohk", [P, RING, K, KEY], F16)
            ohj = bb("ohj", [P, 2, W, NC], F16)
            oht = bb("oht", [P, 2, T, NC], F16)
            eahl = bb("eahl", [P, NC, 2 * DE + 1], F16)
            ki = bb("ki", [P, 2, WG, K], I32)
            kf = bb("kf", [P, 4, WG, K], F32)
            key = bb("key", [P, 2, WG, K], F32)
            pl16 = bb("pl16", [P, 2, WG, K], F16)
            sq = bb("sq", [P, KEY], BF16)
            dl16 = bb("dl16", [P, 2, WG, K], F16)
            tv16 = bb("tv16", [P, WG, K], F16)

        xs = sb("xs", [P, T, D], F32)
        with ExitStack() as layers:
            def lb(name, shape, dt):
                return layers.enter_context(nc.sbuf_tensor(name, shape, dt))

            GH = lb("GH", [P, 2, T, 2 * D], F16)
            plo = lb("plo", [P, 2, 4, D], F32)
            S = lb("S", [P, 2, 4, D], F32)
            V = lb("V", [P, 2, 4, D], F32)
            xc = lb("xc", [P, 2, 4, D], F32)
            z = lb("z", [P, 2, 4, 2 * D], F32)
            zT = lb("zT", [P, 2, 4 * P], F32)
            bst = lb("bst", [D, NB, 6], F32)
            bnv = lb("bnv", [D, 8], F32)
        F = sb("F", [P, T, 4 * S1], F16)
        acc = sb("acc", [P, T, D], F32)
        nadS = sb("nadS", [P, 4 * P], F32)
        Mr = sb("Mr", [P, RB, 4 * P], F16)
        Vg = sb("Vg", [P, 2, 4, S1], F32)
        Vd = sb("Vd", [P, 2, 4, S1], F32)
        r1 = Vg[:].rearrange("p e n c -> p (e n c)").rearrange("p (n c) -> p n c", c=2 * S1)
        c2 = Vd[:].rearrange("p e n c -> p (e n c)").rearrange("p (n c) -> p n c", c=2 * S1)
        q = wts[:, 0:4 * S1].rearrange("p (n c) -> p n c", c=S1)
        rd = sb("rd", [P, 4], F32)
        heads = sb("heads", [P, H, 5, T], F32)
        hd = sb("hd", [P, 6, T], F32)
        asad = acc[:].rearrange("p t d -> p (t d)")[:, 0:2 * H * T].rearrange("p (e h t) -> p e h t", e=2, h=H)
        att = z[0:D].rearrange("p s n c -> p (s n c)")[:, 0:2 * H * D].rearrange("p (e h d) -> p e h d", e=2, h=H)
        wadb = sb("wadb", [D, P], F32)
        wgh = wts[0:D, 5 * D:6 * D]
        amax = sb("amax", [P, 2, 2 * H], F32)
        Cs = C[:].rearrange("p t j -> p (t j)")
        place = [0]

        def gb(n, dt):
            a = place[0]
            place[0] += n * (1 if dt == F16 else 2)
            place[0] += place[0] % 2
            v_ = Cs[:, a:a + n * (1 if dt == F16 else 2)]
            return v_ if dt == F16 else v_.bitcast(dt)
        g_iota = gb(TP, F32)
        g_jid = gb(T, F32)
        g_zero = gb(512, F16)
        g_ohd = gb(TP, F16)
        g_ohs = gb(TP, F16)
        g_oh32 = gb(TP, F32)
        g_raw = gb(DE + 2, I32)
        g_sd = gb(2, F32)
        g_ea = gb(2 * DE + 2, F16)
        g_one = gb(2, F16)
        g_tmp = gb(DE, F32)
        g_rows = gb(2 * D, F16)
        g_tabs = gb(T * GS, F32).rearrange("p (t c) -> p t c", c=GS)
        g_tabd = gb(T * 2 * H, F32).rearrange("p (t c) -> p t c", c=2 * H)
        g_rs = gb(GS, F32)
        g_rd = gb(2 * H, F32)
        g_R = gb(H * GE, F32).rearrange("p (h e) -> p h e", h=H)
        g_D = gb(GE, F32)
        g_pen = gb(GE, F32)
        g_val = gb(H * GE, F32).rearrange("p (h e) -> p h e", h=H)
        g_mx = gb(H, F32)
        g_nm = gb(T * H, F32).rearrange("p (t h) -> p t h", h=H)
        g_w = gb(4 * H, F32)
        g_rhs = gb(S1, F32)
        g_ws = gb(3 * T * H, F32).rearrange("p (a t h) -> p a t h", a=3, h=H)
        g_num = gb(T * S1, F32).rearrange("p (t c) -> p t c", c=S1)
        g_t2 = gb(T * D, F32).rearrange("p (t c) -> p t c", c=D)
        assert place[0] <= T * TP
        gh_d = nc.dram_tensor("gh_d", (TP, 2 * D), F16).ap()
        ts_d = nc.dram_tensor("ts_d", (TP, GS), F32).ap()
        td_d = nc.dram_tensor("td_d", (TP, 2 * H), F32).ap()

        bank = ps("bank", [P, 8, 512])
        pk = [bank[:, i] for i in range(RING)]
        pdeg = bank[:, 3]
        pea = [bank[:, 4 + i] for i in range(2)]
        pf = bank[:, 6:8].rearrange("p a b -> p (a b)")

        s_first = sem("s_first")
        s_firstf = sem("s_firstf")
        s_firstb = sem("s_firstb")
        s_iota = sem("s_iota")
        s_ones = sem("s_ones")
        s_rowidx = sem("s_rowidx")
        s_rows = sem("s_rows")
        s_start = sem("s_start")
        s_startd = sem("s_startd")
        s_startrow = sem("s_startrow")
        s_raw = [sem(f"s_raw{i}") for i in range(2)]
        s_keys = sem("s_keys")
        s_ohjt = sem("s_ohjt")
        s_oh = sem("s_oh")
        s_sq = sem("s_sq")
        s_keyed = sem("s_keyed")
        s_deg = sem("s_deg")
        s_ohused = sem("s_ohused")
        s_evict = sem("s_evict")
        s_chk = sem("s_chk")
        s_chks = sem("s_chks")
        s_wsq = sem("s_wsq")
        s_flag = sem("s_flag")
        s_wsqs = sem("s_wsqs")
        s_flag3 = sem("s_flag3")
        s_v3 = sem("s_v3")
        g_cst = sem("g_cst")
        g_load = sem("g_load")
        g_oh = sem("g_oh")
        g_done = sem("g_done")
        g_gath = [sem(f"g_gath{j}") for j in range(4)]

        AGO = WG
        HALVES = ((0, 6), (6, WG))
        KEYED = (2, 3, 4, 5, 9)

        def back(w):
            return RING if w >= RING else max(k for k in range(WG) if k % RING == w) * -1 + WG + w

        def attrs(par, w0, w1_):
            return raw[:, par].bitcast(F32).rearrange("p w (k c) -> p (w k) c", k=K)[:, w0 * K:w1_ * K, 2:]

        def by_act(b, t):
            return t % 5 != 3 if b < NB - 1 else t % 2 == 0

        STEPS = sum(by_act(b, t) for b in range(NB) for t in range(T))

        def gathered(kk, i=None):
            return (g_gath[2 + (kk - 8) // 4], (kk - 8) % 4) if i is None else (g_gath[kk], i)

        g_gathd = sem("g_gathd")
        g_tab = sem("g_tab")
        g_close = sem("g_close")
        g_taken = sem("g_taken")
        g_load3 = sem("g_load3")
        g_done3 = sem("g_done3")
        g_tab3 = sem("g_tab3")
        g_cst3 = sem("g_cst3")
        g_gaths = sem("g_gaths")
        g_oh3 = sem("g_oh3")
        g_close3 = sem("g_close3")
        g_pad = sem("g_pad")
        g_vA = sem("g_vA")
        g_vH = sem("g_vH")
        g_vX = sem("g_vX")
        g_vM = sem("g_vM")
        g_vS = sem("g_vS")
        g_vT = sem("g_vT")
        g_xw = sem("g_xw")
        g_xwt = sem("g_xwt")
        g_tabs_r = sem("g_tabs_r")
        g_tabd_r = sem("g_tabd_r")
        g_R_r = sem("g_R_r")
        g_Rp = sem("g_Rp")
        g_mxd = sem("g_mxd")
        g_wa = sem("g_wa")
        g_we = sem("g_we")
        g_acc = sem("g_acc")
        s_w = sem("s_w")
        s_x = sem("s_x")
        s_xpad = sem("s_xpad")
        s_cst = sem("s_cst")
        s_t7 = sem("s_t7")
        s_t7r = sem("s_t7r")
        s_dmax = sem("s_dmax")
        s_dsq = sem("s_dsq")
        s_nrm = sem("s_nrm")
        s_gh = sem("s_gh")
        s_agg = sem("s_agg")
        s_plo = sem("s_plo")
        s_free = sem("s_free")
        s_xc = sem("s_xc")
        s_xcu = sem("s_xcu")
        s_var = sem("s_var")
        s_sd = sem("s_sd")
        s_o = sem("s_o")
        s_m7 = sem("s_m7")
        s_oT = sem("s_oT")
        s_h = sem("s_h")
        s_hT = sem("s_hT")
        s_bnv = sem("s_bnv")
        s_bnsd = sem("s_bnsd")
        s_bn = sem("s_bn")
        s_row1 = sem("s_row1")
        s_relu = sem("s_relu")
        s_y = sem("s_y")
        s_x3 = sem("s_x3")
        s_asad = sem("s_asad")
        s_selfl = sem("s_selfl")
        s_am = sem("s_am")
        s_A = sem("s_A")
        s_arg = sem("s_arg")
        s_exp = sem("s_exp")
        s_heads = sem("s_heads")
        s_hd = sem("s_hd")
        s_wh = sem("s_wh")
        s_xw = sem("s_xw")
        s_vg = sem("s_vg")
        s_vhi = sem("s_vhi")
        s_step = sem("s_step")
        s_F = sem("s_F")
        s_S = sem("s_S")
        s_post = sem("s_post")
        s_nad = sem("s_nad")
        s_nads = sem("s_nads")
        s_table = sem("s_table")
        s_steep = sem("s_steep")
        s_M = sem("s_M")
        s_Mu = sem("s_Mu")
        s_c2 = sem("s_c2")
        s_ring = sem("s_ring")
        s_fin = sem("s_fin")
        s_eaev = sem("s_eaev")
        s_degacc = sem("s_degacc")
        s_hi = sem("s_hi")
        s_dif = sem("s_dif")
        s_lo = sem("s_lo")
        s_v = sem("s_v")
        s_g = sem("s_g")
        s_out = sem("s_out")

        block = ctx.enter_context(nc.Block())

        @block.sync
        def _(sp):
            sp.dma_start(fs[0:1, 0:R].bitcast(I32), dst.rearrange("(r c) -> c r", c=ROW)[0:1, :], allow_slow_non_contiguous=True).then_inc(s_first, 16)
            sp.wait_ge(s_start, 1)
            sp.dma_start(starts_d.ap().rearrange("(p b) -> p b", b=2), st_i[:]).then_inc(s_startd, 16)
            sp.wait_ge(s_startd, 16)
            sp.dma_start(starts_row[:], starts_d.ap()[None, :]).then_inc(s_startrow, 16)
            sp.wait_ge(s_startrow, 16)

            def load_group(g, par):
                for w in range(WG):
                    s = sp.value_load(starts_row[0:1, bass.ds(g * WG + w, 1)], min_val=0, max_val=E - SLOT)
                    sp.dma_start(raw[:, par, w, :], edges[bass.ds(s, SLOT), :].rearrange("(p k) c -> p (k c)", k=K)).then_inc(s_raw[par], 16)
            for g in range(2):
                load_group(g, g)
            with sp.Fori(0, G // 2 - 1) as i:
                for par in range(2):
                    g = i * 2 + (2 + par)
                    sp.wait_ge(s_lo, g * 2 - 2)
                    load_group(g, par)
            sp.wait_ge(s_degacc, 1)
            sp.wait_ge(s_lo, 2 * G)
            sp.wait_ge(s_xpad, 1)
            sp.dma_start(xs[:, 0:T - 1, :], x[0:(T - 1) * P, :].rearrange("(t p) d -> p t d", p=P)).then_inc(s_x, 16)
            sp.dma_start(xs[0:LAST, T - 1, :], x[(T - 1) * P:N, :]).then_inc(s_x, 16)
            for e, a_ in enumerate((att_s, att_d)):
                sp.dma_start(att[:, e], a_.to_broadcast([D, H, D])).then_inc(s_x, 16)
            sp.wait_ge(s_flag, 1)
            dense = sp.value_load(flag[0:1, 0:1], min_val=0, max_val=1)

            def chunks(scan):
                with sp.Fori(0, GC) as ch:
                    sp.wait_ge(g_done, scan * GC + (ch + 1))
                    sp.dma_start(g_raw[0:GE, :], edges[bass.ds(ch * GE, GE), :]).then_inc(g_load, 16)

            with sp.If(dense == 0):
                sp.wait_ge(g_cst, 5)
                chunks(0)

            def general_hop(kk, par):
                with sp.If(dense == 0):
                    sp.wait_ge(s_gh, kk * NB + NB)
                    sp.dma_start(gh_d.rearrange("(t p) c -> p t c", p=P), GH[:, par]).then_inc(g_tab, 16)
                    sp.wait_ge(g_tab, kk * 16 + 16)
                    sp.sem_inc(g_pad, 1)
                    chunks(kk + 1)
            with sp.Fori(0, 4) as i:
                for par in range(2):
                    general_hop(i * 2 + par, par)
            for kk in range(8, 13):
                general_hop(kk, kk % 2)
            sp.wait_ge(s_flag3, 1)
            dense3 = sp.value_load(flag[0:1, 1:2], min_val=0, max_val=1)
            with sp.If(dense3 == 0):
                sp.wait_ge(g_tabs_r, 1)
                sp.dma_start(ts_d.rearrange("(t p) c -> p t c", p=P), g_tabs).then_inc(g_tab3, 16)
                sp.wait_ge(g_tab3, 16)
                with sp.Fori(0, GC) as ch:
                    sp.wait_ge(g_done3, ch + 1)
                    sp.dma_start(g_raw[0:GE, :], edges[bass.ds(ch * GE, GE), :]).then_inc(g_load3, 16)
                sp.wait_ge(g_tabd_r, 1)
                sp.dma_start(td_d.rearrange("(t p) c -> p t c", p=P), g_tabd).then_inc(g_tab3, 16)
                sp.wait_ge(g_tab3, 32)
                with sp.Fori(0, H) as h:
                    with sp.Fori(0, GC) as ch:
                        sp.wait_ge(g_done3, h * GC + (ch + (GC + 1)))
                        sp.dma_start(g_raw[0:GE, :], edges[bass.ds(ch * GE, GE), :]).then_inc(g_load3, 16)
            for b, (t0, n) in enumerate(BL):
                sp.wait_ge(s_fin, b + 1)
                if t0 + n == T:
                    if n > 1:
                        sp.dma_start(out[t0 * P:(T - 1) * P, :].rearrange("(t p) d -> p t d", p=P), acc[:, t0:T - 1, :]).then_inc(s_out, 16)
                    sp.dma_start(out[(T - 1) * P:N, :], acc[0:LAST, T - 1, :]).then_inc(s_out, 16)
                else:
                    sp.dma_start(out[t0 * P:(t0 + n) * P, :].rearrange("(t p) d -> p t d", p=P), acc[:, t0:t0 + n, :]).then_inc(s_out, 16)
            sp.wait_ge(s_out, 16 * NB)

        @block.gpsimd
        def _(pool):
            pool.memset(ones[:], 1.0).then_inc(s_ones, 1)
            pool.memset(onesP[:], 1.0).then_inc(s_ones, 1)
            pool.memset(ident[:], 0.0).then_inc(s_g, 1)
            pool.memset(row64[:], 0.0).then_inc(s_g, 1)
            pool.memset(eps_c[:], EPS).then_inc(s_cst, 1)
            pool.wait_ge(s_g, 2)
            pool.affine_select(out=ident[:], in_=ident[:], compare_op=ALU.not_equal, fill=1.0, base=0, pattern=[[-1, P]], channel_multiplier=1).then_inc(s_cst, 1)
            pool.wait_ge(s_cst, 2)
            pool.memset(row64[D:S1, :], 1.0).then_inc(s_cst, 1)
            pool.wait_ge(s_cst, 3)
            pool.tensor_copy(ident16[:], ident[:]).then_inc(s_cst, 1)
            pool.iota(wlo[:], pattern=[[W, 2]], base=0, channel_multiplier=2 * W, allow_small_or_imprecise_dtypes=True).then_inc(s_iota, 1)
            pool.iota(iota_p[:], pattern=[[1, P], [0, K]], base=0, channel_multiplier=0, allow_small_or_imprecise_dtypes=True).then_inc(s_iota, 1)
            pool.iota(iota_key[:], pattern=[[1, T], [T, W]], base=0, channel_multiplier=0, allow_small_or_imprecise_dtypes=True).then_inc(s_iota, 1)
            pool.iota(iota_j[:], pattern=[[1, W], [0, NC]], base=0, channel_multiplier=0, allow_small_or_imprecise_dtypes=True).then_inc(s_iota, 1)
            pool.iota(iota_t[:], pattern=[[1, T], [0, NC]], base=1, channel_multiplier=0, allow_small_or_imprecise_dtypes=True).then_inc(s_iota, 1)
            pool.iota(woff[:], pattern=[[W, WG], [0, K]], base=0, channel_multiplier=0, allow_small_or_imprecise_dtypes=True).then_inc(s_iota, 1)
            pool.wait_ge(s_rowidx, 1)
            for b in range(2):
                pool.indirect_dma_start(out=rows_i[:, b, :], out_offset=None, in_=dst.rearrange("(r c) -> r c", c=ROW),
                                        in_offset=bass.IndirectOffsetOnAxis(ap=row_i[:, b:b + 1], axis=0)).then_inc(s_rows, 16)
            pool.memset(C[:, :, NW:TP], 0.0).then_inc(s_iota, 1)
            pool.memset(eaT[:, NW:TP], 0.0).then_inc(s_iota, 1)
            pool.memset(eahl[:, :, 2 * DE:2 * DE + 1], 1.0).then_inc(s_iota, 1)
            pool.wait_ge(s_iota, 9)
            with pool.Fori(0, G // 2) as i:
                for par in range(2):
                    g = i * 2 + par
                    for half, (w0, w1_) in enumerate(HALVES):
                        pool.wait_ge(s_hi, g * 2 + (half + 1))
                        pool.tensor_tensor(attrs(par, w0, w1_), attrs(par, w0, w1_), eahl[:, w0 * K:w1_ * K, 0:DE], ALU.subtract).then_inc(s_dif, 1)

            pool.wait_ge(s_degacc, 1)
            pool.wait_ge(s_lo, 2 * G)
            pool.memset(xs[:, T - 1, :], 0.0).then_inc(s_xpad, 1)
            pool.wait_ge(s_x, 64)

            def side(kk, b):
                t0, n = BL[b]
                m = kk * NB + b
                pool.wait_ge(s_xcu, m + (1 + (b == 0)))
                pool.tensor_tensor(xc[:, b % 2, 0:n, :], xs[:, t0:t0 + n, :], nrm[:, 3, t0:t0 + n, None].to_broadcast([P, n, D]), ALU.mult).then_inc(s_xc, 1)
            pool.wait_ge(s_flag, 1)
            dense = pool.value_load(flag[0:1, 0:1], min_val=0, max_val=1)

            def general_consts(done):
                pool.iota(g_iota, pattern=[[1, TP]], base=0, channel_multiplier=0, allow_small_or_imprecise_dtypes=True).then_inc(done, 1)
                pool.iota(g_jid, pattern=[[P, T]], base=0, channel_multiplier=1, allow_small_or_imprecise_dtypes=True).then_inc(done, 1)
                pool.memset(g_zero, 0.0).then_inc(done, 1)
                pool.memset(g_one, 1.0).then_inc(done, 1)
                pool.memset(g_ea, 1.0).then_inc(done, 1)
            with pool.If(dense == 0):
                general_consts(g_cst)
            pool.wait_ge(s_nrm, 1)

            def general_hop(kk, which):
                with pool.If(dense == 0):
                    pool.wait_ge(g_tab, kk * 16 + 16)
                    pool.sem_inc(g_pad, 1)
                    with pool.Fori(0, GC) as ch:
                        pool.wait_ge(g_load, (kk + 1) * (16 * GC) + (ch * 16 + 16))
                        pool.sem_inc(g_pad, 1)
                        pool.indirect_dma_start(out=g_rows[0:GE, :], out_offset=None, in_=gh_d,
                                                in_offset=bass.IndirectOffsetOnAxis(ap=g_raw[0:GE, 0:1], axis=0)).then_inc(which[0], 16)
            with pool.Fori(0, 4) as i:
                for par in range(2):
                    general_hop(i * 2 + par, gathered(par, i))
                    for b in range(NB):
                        side(i * 2 + par, b)
            general_hop(8, gathered(8))
            for b in range(NB):
                side(8, b)
            general_hop(9, gathered(9))
            general_hop(10, gathered(10))
            pool.wait_ge(s_m7, NB)
            pool.wait_ge(s_xc, 9 * NB)
            pool.memset(eaT[D:S1, :], 1.0).then_inc(s_row1, 1)
            pool.wait_ge(s_row1, 1)
            general_hop(11, gathered(11))
            general_hop(12, gathered(12))
            for b, (t0, n) in enumerate(BL):
                m = 9 * NB + b
                pool.wait_ge(s_free, 12 * NB + b + 1)
                if b >= 2:
                    pool.wait_ge(s_y, NB + b - 1)
                    pool.wait_ge(s_xcu, m + 1)
                pool.tensor_copy(z[:, b % 2, 0:n, D:2 * D], xs[:, t0:t0 + n, :]).then_inc(s_g, 1)
                pool.tensor_tensor(xc[:, b % 2, 0:n, :], xs[:, t0:t0 + n, :], biases[:, 0:1, :].to_broadcast([P, n, D]), ALU.add).then_inc(s_g, 1)
                pool.wait_ge(s_g, 2 + 3 * b + 2)
                pool.tensor_tensor(xc[:, b % 2, 0:n, :], xc[:, b % 2, 0:n, :], biases[:, 1:2, :].to_broadcast([P, n, D]), ALU.add).then_inc(s_g, 1)
                pool.wait_ge(s_g, 2 + 3 * b + 3)
                pool.sem_inc(s_xc, 1)
            pool.wait_ge(s_am, 1)
            pool.partition_all_reduce(amax[:, 1, :], amax[:, 0, :], P, bass.bass_isa.ReduceOp.max).then_inc(s_A, 1)
            pool.wait_ge(s_flag3, 1)
            dense3 = pool.value_load(flag[0:1, 1:2], min_val=0, max_val=1)
            with pool.If(dense3 == 1):
                with pool.Fori(0, H) as h:
                    pool.wait_ge(s_nad, h * NB + 1)
                    pool.tensor_copy(wgh[:], wg[:, bass.ds(h, 1), :].rearrange("p o d -> p (o d)")).then_inc(s_wh, 1)
                    pool.tensor_copy(wadb[:], nwa[:, bass.ds(h, 1)].to_broadcast([D, P])).then_inc(s_wh, 1)
            with pool.Else():
                pool.wait_ge(s_agg, 13 * NB)
                general_consts(g_cst3)
                pool.wait_ge(g_tab3, 16)
                with pool.Fori(0, GC) as ch:
                    pool.wait_ge(g_load3, ch * 16 + 16)
                    pool.sem_inc(g_pad, 1)
                    pool.indirect_dma_start(out=g_rs[0:GE, :], out_offset=None, in_=ts_d,
                                            in_offset=bass.IndirectOffsetOnAxis(ap=g_raw[0:GE, 0:1], axis=0)).then_inc(g_gaths, 16)
                pool.wait_ge(g_tab3, 32)
                with pool.Fori(0, H) as h:
                    with pool.Fori(0, GC) as ch:
                        pool.wait_ge(g_load3, h * (16 * GC) + (ch * 16 + (16 * GC + 16)))
                        pool.sem_inc(g_pad, 1)
                        pool.indirect_dma_start(out=g_rs[0:GE, :], out_offset=None, in_=ts_d,
                                                in_offset=bass.IndirectOffsetOnAxis(ap=g_raw[0:GE, 0:1], axis=0)).then_inc(g_gaths, 16)
                        pool.indirect_dma_start(out=g_rd[0:GE, :], out_offset=None, in_=td_d,
                                                in_offset=bass.IndirectOffsetOnAxis(ap=g_raw[0:GE, 1:2], axis=0)).then_inc(g_gathd, 16)

        @block.scalar
        def _(act):
            act.sem_inc(s_evict, AGO)
            for o_, i_ in ((weS[0:DE, :], We), (weS[DE:2 * DE, :], We), (weS[2 * DE:S1, :], be[None, :]), (w1[:], W1), (w2[0:D, :], W2),
                           (w2[D:S1, :], b2[None, :]), (wlr[:, 0:D], Wl), (wlr[:, D:2 * D], Wr), (wg[:], Wg.rearrange("k (h d) -> k h d", h=H)),
                           (biases[:, 0], bl[None, :].to_broadcast([P, D])), (biases[:, 1], br[None, :].to_broadcast([P, D])),
                           (biases[:, 2], bias_g[None, :].to_broadcast([P, D]))):
                act.dma_start(o_, i_).then_inc(s_w, 16)
            for j_, i_ in enumerate((b1, gamma, beta)):
                act.dma_start(vecs[:, j_:j_ + 1], i_[:, None]).then_inc(s_w, 16)
            WL = 15 * 16
            act.wait_ge(s_iota, 9)

            def high_attrs(i, k, half):
                w0, w1_ = HALVES[half]
                act.wait_ge(s_raw[k % 2], i * (16 * WG) + 16 * WG * (k // 2 + 1))
                act.activation(eahl[:, w0 * K:w1_ * K, 0:DE], attrs(k % 2, w0, w1_), ACT.Copy).then_inc(s_hi, 1)

            def low_attrs(i, k, half):
                w0, w1_ = HALVES[half]
                act.wait_ge(s_dif, i * 4 + (k * 2 + half + 1))
                act.activation(eahl[:, w0 * K:w1_ * K, DE:2 * DE], attrs(k % 2, w0, w1_), ACT.Copy, scale=LO).then_inc(s_lo, 1)

            def one_hot(i, par, w):
                r = w % RING
                n_ = i * (2 * len(KEYED)) + (par * len(KEYED) + KEYED.index(w) + 1)
                act.wait_ge(s_keys, i * 2 + (par + 1))
                act.wait_ge(s_keyed, n_)
                act.activation(sq[:], iota_key[:].rearrange("p t j -> p (t j)"), ACT.Square, bias=key[:, par, w, K - 1:K], scale=-1.0).then_inc(s_sq, 1)
                act.wait_ge(s_sq, n_)
                act.wait_ge(s_ohused, i * (2 * WG) + (par * WG + w + 1 + AGO - back(w)))
                act.activation(ohk[:, r, K - 1], sq[:], ACT.Relu, bias=onesP[:], scale=-1.0).then_inc(s_keyed, 1)

            def evict(i, par, w):
                wi = i * (2 * WG) + (par * WG + w)
                act.wait_ge(s_ohused, wi + (AGO + 1))
                act.activation(C[:, :, bass.ds(wi * W, W)], pk[w % RING][:, 0:KEY].rearrange("p (t j) -> p t j", j=W), ACT.Copy).then_inc(s_evict, 1)

            def build_group(i, par, more):
                for w in range(WG):
                    if w in KEYED:
                        one_hot(i, par, w)
                    if w >= 1:
                        evict(i, par, w - 1)
                    if w == 2:
                        low_attrs(i, par, 1)
                    if more and w == HALVES[0][1]:
                        high_attrs(i, par + 1, 0)
                    if more and w == HALVES[0][1] + 2:
                        low_attrs(i, par + 1, 0)
                evict(i, par, WG - 1)
                act.activation(eaT[:, bass.ds((i * 2 + par) * (WG * W), WG * W)], pea[par][0:65, 0:WG * W], ACT.Copy).then_inc(s_eaev, 1)
                if more:
                    high_attrs(i, par + 1, 1)

            act.sem_inc(s_keyed, 1)
            high_attrs(0, 0, 0)
            low_attrs(0, 0, 0)
            high_attrs(0, 0, 1)
            with act.Fori(0, G // 2 - 1) as i:
                for par in range(2):
                    build_group(i, par, True)
            build_group(G // 2 - 1, 0, True)
            build_group(G // 2 - 1, 1, False)

            def low(kk, b, extra=0):
                t0, n = BL[b]
                act.wait_ge(s_agg, kk * NB + (b + 1))
                if isinstance(kk, int) and kk >= 10:
                    if b >= 2 and kk != 11:
                        act.wait_ge(s_o, (kk - 10) // 2 * NB + b - 1)
                    elif kk == 11 and b < 2:
                        act.wait_ge(s_o, NB)
                    else:
                        act.wait_ge(s_free, kk * NB + NB + b - 1 + (b == 0))
                else:
                    act.wait_ge(s_free, kk * NB + (NB + b - 1 + (b == 0)))
                act.activation(plo[:, b % 2, 0:n, :], bank[:, b, 0:n * 2 * D].rearrange("p (t c) -> p t c", c=2 * D)[:, :, D:2 * D], ACT.Copy, scale=1.0 / LO).then_inc(s_plo, 1)

            def root(m, n):
                act.wait_ge(s_var, m + 1)
                act.activation(sd[:, 0:n], mv[:, 0:n, 1], ACT.Sqrt, bias=eps_c[:]).then_inc(s_sd, 1)

            act.wait_ge(s_dmax, 1)
            act.activation(nrm[:, 0:2, :], nrm[:, 2:4, :], ACT.Sqrt).then_inc(s_dsq, 1)
            with act.Fori(0, 4) as i:
                for par in range(2):
                    for b in range(NB):
                        low(i * 2 + par, b)
            for b in range(NB):
                low(8, b)
            for b in range(NB):
                low(9, b)
                root(b, BL[b][1])
            def l1_take(b):
                t0, n = BL[b]
                act.wait_ge(s_m7, b + 1)
                act.activation(zT[0:D, b % 2, 0:n * P], bank[0:D, 7, 0:n * P], ACT.Copy).then_inc(s_oT, 1)

            def l1_take2(b):
                t0, n = BL[b]
                act.wait_ge(s_h, b + 1)
                act.activation(eaT[0:D, t0 * P:(t0 + n) * P], bank[0:D, b, 0:n * P], ACT.Identity, bias=vecs[:, 0:1]).then_inc(s_hT, 1)
            for b in range(NB + 2):
                if b < NB:
                    low(10, b)
                if 1 <= b <= NB:
                    l1_take(b - 1)
                if b >= 2:
                    l1_take2(b - 2)
            act.wait_ge(s_bnv, 1)
            act.activation(bnv[:, 2:3], bnv[:, 1:2], ACT.Sqrt, bias=eps_c[0:D, :]).then_inc(s_bnsd, 1)
            act.wait_ge(s_bn, 1)
            for b, (t0, n) in enumerate(BL):
                act.activation(eaT[0:D, t0 * P:(t0 + n) * P], eaT[0:D, t0 * P:(t0 + n) * P], ACT.Relu, bias=bnv[:, 5:6], scale=bnv[:, 4:5]).then_inc(s_relu, 1)
                if b >= 1:
                    root(NB + b - 1, BL[b - 1][1])
            root(2 * NB - 1, BL[-1][1])
            for b in range(NB):
                low(11, b)

            def l2_take(b):
                n = BL[b][1]
                act.wait_ge(s_m7, NB + b + 1)
                act.activation(zT[:, b % 2, 0:n * P], bank[:, 7, 0:n * P], ACT.Copy).then_inc(s_oT, 1)
            for b in range(NB + 2):
                if b < NB:
                    low(12, b)
                if 1 <= b <= NB:
                    l2_take(b - 1)
                if b >= 2:
                    root(2 * NB + b - 2, BL[b - 2][1])
            for b, (t0, n) in enumerate(BL):
                act.wait_ge(s_m7, 2 * NB + b + 1)
                act.activation(eaT[0:D, t0 * P:(t0 + n) * P], bank[0:D, 7, 0:n * P], ACT.Copy).then_inc(s_oT, 1)
            act.wait_ge(s_flag3, 1)
            dense3 = act.value_load(flag[0:1, 1:2], min_val=0, max_val=1)
            with act.If(dense3 == 1):
                act.wait_ge(s_arg, 1)
                act.activation(heads[:, :, 1:5, :], heads[:, :, 1:5, :], ACT.Exp).then_inc(s_exp, 1)
                with act.Fori(0, H) as h:
                    act.activation(small[0:1, 62:63], onesP[0:1, :], ACT.Sigmoid).then_inc(s_table, 1)
                    act.wait_ge(s_ring, h * T + 1)
                    for b, (t0, n) in enumerate(BL):
                        for e in range(2):
                            act.wait_ge(s_vg, h * (2 * NB) + (2 * b + e + 1))
                            act.activation(F[:, t0:t0 + n, 2 * S1 * e:2 * S1 * e + D], (Vg, Vd)[e][:, b % 2, 0:n, 0:D], ACT.Copy, scale=1.0 / LO).then_inc(s_vhi, 1)

                    act.wait_ge(s_steep, h + 1)

                    def take(b):
                        t0, n = BL[b]
                        act.wait_ge(s_Mu, h * (NB * T) + ((b + 1) * T + RB))
                        act.wait_ge(s_post, h * NB + (b + 1))
                        for jj in range(n):
                            t = t0 + jj
                            act.activation(c2[:, jj], bank[:, t % RB, 4 * S1:6 * S1], ACT.Copy).then_inc(s_c2, 1)
                            act.activation(r1[:, jj], bank[:, t % RB, 0:2 * S1], ACT.Identity, scale=hd[:, 3, t:t + 1]).then_inc(s_c2, 1)

                    for b, (t0, n) in enumerate(BL):
                        act.wait_ge(s_nad, h * NB + (b + 2))
                        for t in range(T):
                            mi = b * T + t
                            if t == 2:
                                if b >= 1:
                                    act.wait_ge(s_M, h * (NB * T) + b * T)
                                act.activation(nadS[:, 0:n * P], bank[:, 5 + b % 2, 0:n * P], ACT.Copy).then_inc(s_nads, 1)
                            if t == RB - 1 and b >= 1:
                                take(b - 1)
                            if by_act(b, t):
                                act.wait_ge(s_Mu, h * (NB * T) + (mi + 1))
                                act.activation(Mr[:, mi % RB, 0:n * P], bank[:, 5 + b % 2, 0:n * P], ACT.Sigmoid, bias=hd[:, 5, t:t + 1], scale=-STEEP).then_inc(s_step, 1)
                    take(NB - 1)
            with act.Else():
                act.wait_ge(g_wa, 1)
                act.activation(g_ws[:, 2], g_ws[:, 1], ACT.Exp).then_inc(g_we, 1)
                with act.Fori(0, H) as h:
                    with act.Fori(0, GC) as ch:
                        act.wait_ge(g_wa, h * GC + (ch + 2))
                        act.activation(g_w[0:GE, 3 * H:4 * H], g_w[0:GE, 2 * H:3 * H], ACT.Exp).then_inc(g_we, 1)
            for b, (t0, n) in enumerate(BL):
                root(3 * NB + b, n)

        @block.vector
        def _(v):
            c = Count(v, s_v)
            v.wait_ge(s_first, 16)
            c.add(v.tensor_copy(first_f, fs[0:1, 0:R].bitcast(I32)))
            c.here()
            v.tensor_scalar(first_f, first_f, 0.0, None, ALU.add).then_inc(s_firstf, 1)
            v.wait_ge(s_firstb, 1)
            v.wait_ge(s_iota, 6)
            c.add(v.tensor_copy(fb[:], pf[:, 0:R]))
            c.here()
            for b in range(2):
                c.add(v.tensor_scalar(fs[:], fb[:], wlo[:, b:b + 1], None, ALU.is_lt, ALU.add, accum_out=cnt[:, b:b + 1]))
                c.here()
            c.add(v.tensor_scalar(cnt[:, 2:4], cnt[:, 0:2], -1.0, 0.0, ALU.add, ALU.max))
            c.here()
            v.tensor_copy(row_i[:], cnt[:, 2:4]).then_inc(s_rowidx, 1)
            v.wait_ge(s_rows, 32)
            for b in range(2):
                c.add(v.tensor_copy(fb[:, b * ROW:(b + 1) * ROW], rows_i[:, b]))
                c.here()
                c.add(v.tensor_scalar(fs[:, 0:ROW], fb[:, b * ROW:(b + 1) * ROW], wlo[:, b:b + 1], None, ALU.is_lt, ALU.add, accum_out=cnt[:, 4 + b:5 + b]))
                c.here()
            c.add(v.scalar_tensor_tensor(cnt[:, 6:8], cnt[:, 2:4], float(ROW), cnt[:, 4:6], ALU.mult, ALU.add))
            c.here()
            c.add(v.tensor_scalar(cnt[:, 0:2], cnt[:, 6:8], float(E - SLOT), None, ALU.min))
            c.here()
            v.tensor_copy(st_i[:], cnt[:, 0:2]).then_inc(s_start, 1)

            def keys(i, k, step):
                par = k % 2
                edge = raw[:, par].rearrange("p w (k c) -> p w k c", k=K)
                kd, kt, ok = kf[:, 0], kf[:, 1], kf[:, 2]
                c.here()
                if step == 0:
                    v.wait_ge(s_raw[par], i * (16 * WG) + 16 * WG * (k // 2 + 1))
                    c.add(v.tensor_scalar(ki[:, 0], edge[:, :, :, 0], 7, None, ALU.arith_shift_right))
                    c.add(v.tensor_scalar(ki[:, 1], edge[:, :, :, 0], 127, None, ALU.bitwise_and))
                    c.add(v.tensor_tensor(kd, edge[:, :, :, 1], woff[:], ALU.subtract))
                elif step == 1:
                    c.add(v.tensor_copy(kt, ki[:, 0]))
                    c.add(v.tensor_copy(pl16[:, par], ki[:, 1]))
                    c.add(v.tensor_copy(dl16[:, par], kd))
                    c.add(v.tensor_scalar(ok, kd, 0.0, None, ALU.is_ge))
                    c.add(v.tensor_scalar(woff[:], woff[:], float(W * WG), None, ALU.add))
                elif step == 2:
                    c.add(v.scalar_tensor_tensor(key[:, par], kd, float(T), kt, ALU.mult, ALU.add))
                    c.add(v.tensor_tensor(ohj[:, par], iota_j[:], dl16[:, par].rearrange("p w k -> p (w k)")[:, None, :].to_broadcast([P, W, NC]), ALU.is_equal))
                    c.add(v.scalar_tensor_tensor(kf[:, 3], kd, W - 0.5, ok, ALU.is_lt, ALU.mult))
                elif step == 3:
                    c.add(v.scalar_tensor_tensor(tv16[:], kt, 1.0, kf[:, 3], ALU.add, ALU.mult))
                else:
                    v.tensor_tensor(oht[:, par], iota_t[:], tv16[:].rearrange("p w k -> p (w k)")[:, None, :].to_broadcast([P, T, NC]), ALU.is_equal).then_inc(s_keys, 1)

            def build_group(i, par, more):
                for w in range(WG):
                    r = w % RING
                    v.wait_ge(s_ohused, i * (2 * WG) + (par * WG + w + 1 + AGO - back(w)))
                    v.tensor_tensor(ohp[:, r], iota_p[:], pl16[:, par, w, None, :].to_broadcast([P, P, K]), ALU.is_equal)
                    for k in range(K - (w in KEYED)):
                        last = v.tensor_scalar(ohk[:, r, k], iota_key[:].rearrange("p t j -> p (t j)"), key[:, par, w, k:k + 1], None, ALU.is_equal)
                    last.then_inc(s_oh, 1)
                    if more and 3 <= w < 8:
                        keys(i, par + 1, w - 3)

            for step in range(5):
                keys(0, 0, step)
            v.wait_ge(s_keys, 1)
            with v.Fori(0, G // 2 - 1) as i:
                c.loop(i, 2 * 12)
                for par in range(2):
                    build_group(i, par, True)
                c.end(G // 2 - 1)
            build_group(G // 2 - 1, 0, True)
            build_group(G // 2 - 1, 1, False)
            v.wait_ge(s_deg, 1)
            v.tensor_copy(dego[:], pdeg[:, 0:T]).then_inc(s_degacc, 1)
            v.sem_inc(s_free, NB)
            WL = 15 * 16
            v.wait_ge(s_w, WL)
            v.wait_ge(s_x, 64)
            c.add(v.tensor_scalar(weS[DE:2 * DE, :], weS[DE:2 * DE, :], 1.0 / LO, None, ALU.mult))
            for e in range(2):
                c.add(v.tensor_tensor(att[:, e], att[:, e], wg[:], ALU.mult))
            c.here()
            v.tensor_reduce(wa[:], att[:], AX, ALU.add).then_inc(s_t7r, 1)
            v.wait_ge(s_t7r, 1)
            c.add(v.tensor_scalar(nwa[:], wa[:, 1, :], -1.0, None, ALU.mult))
            c.add(v.tensor_tensor(att[:, 0], wg[:], wg[:], ALU.mult))
            c.here()
            v.tensor_copy(att[:, 1], att[:, 0]).then_inc(s_wsq, 1)
            v.wait_ge(s_t7, 1)
            c.add(v.tensor_scalar(nrm[:, 3, :], bank[:, 7, 0:T], 1.0, None, ALU.max))
            c.add(v.tensor_copy(wlrT[:], bank[:, 7, P:P + D]))
            c.here()
            c.add(v.tensor_scalar(nrm[:, 2, :], dego[:], 1.0, None, ALU.max))
            c.here()
            c.add(v.tensor_reduce(chk[:, 0:1], dego[:], AX, ALU.add))
            c.add(v.tensor_scalar(small[:, 0:T], nrm[:, 3, :], MOST, None, ALU.is_gt))
            c.here()
            v.tensor_reduce(chk[:, 1:2], small[:, 0:T], AX, ALU.add).then_inc(s_chk, 1)
            v.wait_ge(s_chks, 1)
            c.add(v.tensor_scalar(chk1[:, 0:1], bank[0:1, 7, 256:257], float(E), None, ALU.is_equal))
            c.add(v.tensor_scalar(chk1[:, 1:2], bank[0:1, 7, 257:258], 0.0, None, ALU.is_equal))
            c.here()
            c.add(v.tensor_tensor(chk1[:, 2:3], chk1[:, 0:1], chk1[:, 1:2], ALU.mult))
            c.here()
            v.tensor_copy(flag[:, 0:1], chk1[:, 2:3]).then_inc(s_flag, 1)
            v.wait_ge(s_flag, 1)
            dense = v.value_load(flag[0:1, 0:1], min_val=0, max_val=1)

            def ends(done, n_):
                for e in range(2):
                    last = v.tensor_copy(g_sd[0:GE, e:e + 1], g_raw[0:GE, e:e + 1])
                    last.then_inc(done, 1)

            with v.If(dense == 0):
                v.wait_ge(g_cst, 5)
                with v.Fori(0, GC) as ch:
                    v.wait_ge(g_load, ch * 16 + 16)
                    v.wait_ge(g_done, ch + 1)
                    ends(g_vA, 2)
                    ea_ = g_raw[0:GE, 2:].bitcast(F32)
                    v.tensor_copy(g_ea[0:GE, 0:DE], ea_).then_inc(g_vA, 1)
                    v.wait_ge(g_vA, ch * 6 + 3)
                    v.tensor_tensor(g_tmp[0:GE, :], ea_, g_ea[0:GE, 0:DE], ALU.subtract).then_inc(g_vA, 1)
                    v.tensor_scalar(g_ohs[0:GE, :], g_iota[0:GE, :], g_sd[0:GE, 0:1], None, ALU.is_equal).then_inc(g_vA, 1)
                    v.wait_ge(g_vA, ch * 6 + 5)
                    v.tensor_scalar(g_ea[0:GE, DE:2 * DE], g_tmp[0:GE, :], LO, None, ALU.mult).then_inc(g_vA, 1)
                    v.wait_ge(g_vA, ch * 6 + 6)
                    v.tensor_scalar(g_ohd[0:GE, :], g_iota[0:GE, :], g_sd[0:GE, 1:2], None, ALU.is_equal).then_inc(g_oh, 1)
                v.wait_ge(g_close, 1)
                v.tensor_copy(dego[:], bank[:, 7, 0:T]).then_inc(g_taken, 1)
                for b, (t0, n) in enumerate(BL):
                    v.tensor_copy(eaT[:, t0 * P:(t0 + n) * P], bank[0:S1, b, 0:n * P]).then_inc(g_taken, 1)
                v.wait_ge(g_taken, NB + 1)
                v.wait_ge(g_close, 2)
                v.tensor_scalar(nrm[:, 3, :], bank[:, 7, 0:T], 1.0, None, ALU.max).then_inc(g_taken, 1)
                v.tensor_scalar(nrm[:, 2, :], dego[:], 1.0, None, ALU.max).then_inc(g_taken, 1)
                v.wait_ge(g_taken, NB + 3)
            v.sem_inc(s_dmax, 1)

            def general_hop(kk):
                with v.If(dense == 0):
                    with v.Fori(0, GC) as ch:
                        v.wait_ge(g_load, (kk + 1) * (16 * GC) + (ch * 16 + 16))
                        v.wait_ge(g_done, (kk + 1) * GC + (ch + 1))
                        v.tensor_copy(g_sd[0:GE, 1:2], g_raw[0:GE, 1:2]).then_inc(g_vH, 1)
                        v.wait_ge(g_vH, kk * GC + (ch + 1))
                        v.tensor_scalar(g_ohd[0:GE, :], g_iota[0:GE, :], g_sd[0:GE, 1:2], None, ALU.is_equal).then_inc(g_oh, 1)

            v.wait_ge(s_dsq, 1)
            c.add(v.reciprocal(nrm[:, 4:6, :], nrm[:, 0:2, :]))
            c.here()
            ns, nd = nrm[:, 4, :], nrm[:, 5, :]
            c.add(v.tensor_tensor(nrm[:, 6, :], ns, nd, ALU.mult))
            c.add(v.tensor_scalar(nrm[:, 7, :], ns, LO, None, ALU.mult))
            c.add(v.tensor_scalar(nrm[:, 8, :], nd, 0.9, None, ALU.mult))
            c.add(v.tensor_scalar(nrm[:, 9, :], nd, LO, None, ALU.mult))
            c.here()
            c.add(v.tensor_scalar(nrm[:, 2, :], nrm[:, 6, :], 0.9 * LO, None, ALU.mult))
            c.add(v.tensor_tensor(nrm[:, 10, :], nrm[:, 9, :], nd, ALU.mult))
            v.tensor_scalar(nrm[:, 3, :], ns, 0.1 * LO, None, ALU.mult).then_inc(s_nrm, 1)
            v.wait_ge(s_nrm, 1)

            def cols(row, t0, n):
                return nrm[:, row, t0:t0 + n, None].to_broadcast([P, n, D])

            def split(src, par, t0, n):
                c.here()
                c.add(v.tensor_scalar(GH[:, par, t0:t0 + n, 0:D], src, 1.0 / LO, None, ALU.mult))
                c.here()
                v.scalar_tensor_tensor(GH[:, par, t0:t0 + n, D:2 * D], GH[:, par, t0:t0 + n, 0:D], -LO, src, ALU.mult, ALU.add).then_inc(s_gh, 1)

            v.wait_ge(s_x, 64)
            for b, (t0, n) in enumerate(BL):
                if b >= 2:
                    v.wait_ge(s_gh, b - 1)
                c.add(v.tensor_tensor(V[:, b % 2, 0:n, :], xs[:, t0:t0 + n, :], cols(7, t0, n), ALU.mult))
                split(V[:, b % 2, 0:n, :], 0, t0, n)

            def high(b, n):
                return bank[:, b, 0:n * 2 * D].rearrange("p (t c) -> p t c", c=2 * D)[:, :, 0:D]

            def sums(kk, b, frees):
                t0, n = BL[b]
                v.wait_ge(s_plo, kk * NB + (b + 1))
                c.here()
                ins = v.tensor_tensor(S[:, b % 2, 0:n, :], high(b, n), plo[:, b % 2, 0:n, :], ALU.add)
                if frees:
                    ins.then_inc(s_free, 1)
                    v.wait_ge(s_free, kk * NB + (NB + b + 1))
                else:
                    c.add(ins)
                    c.here()
                return S[:, b % 2, 0:n, :]

            def l0_block(kk, b, par):
                t0, n = BL[b]
                s_ = sums(kk, b, True)
                c.add(v.tensor_tensor(s_, s_, cols(2, t0, n), ALU.mult))
                c.here()
                v.wait_ge(s_xc, kk * NB + (b + 1))
                v.wait_ge(s_gh, kk * NB + (NB + b - 1 + (b == 0)))
                v.tensor_tensor(V[:, b % 2, 0:n, :], s_, xc[:, b % 2, 0:n, :], ALU.add).then_inc(s_xcu, 1)
                v.wait_ge(s_xcu, kk * NB + (b + 3))
                split(V[:, b % 2, 0:n, :], par, t0, n)

            v.sem_inc(s_xcu, 2)
            with v.Fori(0, 4) as i:
                c.loop(i, 2 * NB * 2)
                for par in range(2):
                    general_hop(i * 2 + par)
                    for b in range(NB):
                        l0_block(i * 2 + par, b, 1 - par)
                c.end(4)
            general_hop(8)
            for b in range(NB):
                l0_block(8, b, 1)
            general_hop(9)

            def norm(m, y, n, o):
                c.here()
                for j in range(n):
                    c.add(v.bn_stats(small[:, 6 * j:6 * j + 6], y[:, j, :]))
                c.here()
                for j in range(n):
                    last = v.bn_aggr(mv[:, j, :], small[:, 6 * j:6 * j + 6])
                    if j < n - 1:
                        c.add(last)
                last.then_inc(s_var, 1)
                v.wait_ge(s_var, m + 1)
                v.wait_ge(s_sd, m + 1)
                c.add(v.reciprocal(small[:, 32:32 + n], sd[:, 0:n]))
                c.here()
                for j in range(n):
                    last = v.tensor_scalar(o[:, j, :], y[:, j, :], mv[:, j, 0:1], small[:, 32 + j:33 + j], ALU.subtract, ALU.mult)
                    if j < n - 1:
                        c.add(last)
                return last

            for b, (t0, n) in enumerate(BL):
                s_ = sums(9, b, True)
                xb = xs[:, t0:t0 + n, :]
                c.add(v.tensor_tensor(s_, s_, cols(8, t0, n), ALU.mult))
                c.here()
                c.add(v.scalar_tensor_tensor(V[:, b % 2, 0:n, :], xb, 1.1, s_, ALU.mult, ALU.add))
                c.add(norm(b, V[:, b % 2, 0:n, :], n, xb))
                c.here()
                c.add(v.tensor_scalar(V[:, b % 2, 0:n, :], xb, LO, None, ALU.mult))
                split(V[:, b % 2, 0:n, :], 0, t0, n)

            general_hop(10)
            for b in range(NB + 2):
                if b < NB:
                    t0, n = BL[b]
                    s_ = sums(10, b, False)
                    if b >= 2:
                        v.wait_ge(s_m7, b - 1)
                    v.tensor_tensor(z[:, b % 2, 0:n, 0:D], s_, xs[:, t0:t0 + n, :], ALU.add).then_inc(s_o, 1)
                if b >= 2:
                    t0, n = BL[b - 2]
                    v.wait_ge(s_hT, b - 1)
                    last = v.bn_stats(bst[:, b - 2, :], eaT[0:D, t0 * P:min((t0 + n) * P, N)])
                    c.add(last)
            c.here()
            v.bn_aggr(bnv[:, 0:2], bst[:].rearrange("p b s -> p (b s)")).then_inc(s_bnv, 1)
            v.wait_ge(s_bnsd, 1)
            c.add(v.reciprocal(bnv[:, 3:4], bnv[:, 2:3]))
            c.here()
            c.add(v.tensor_tensor(bnv[:, 4:5], bnv[:, 3:4], vecs[:, 1:2], ALU.mult))
            c.here()
            c.add(v.tensor_tensor(bnv[:, 6:7], bnv[:, 0:1], bnv[:, 4:5], ALU.mult))
            c.here()
            v.tensor_tensor(bnv[:, 5:6], vecs[:, 2:3], bnv[:, 6:7], ALU.subtract).then_inc(s_bn, 1)
            for b, (t0, n) in enumerate(BL):
                xb = xs[:, t0:t0 + n, :]
                v.wait_ge(s_y, b + 1)
                v.wait_ge(s_gh, 10 * NB + NB + b - 1 + (b == 0))
                v.tensor_tensor(V[:, b % 2, 0:n, :], bank[:, b, 0:n * D].rearrange("p (t d) -> p t d", d=D), xb, ALU.add).then_inc(s_free, 1)
                v.wait_ge(s_free, NB + 10 * NB + b + 1)
                c.add(norm(NB + b, V[:, b % 2, 0:n, :], n, xb))
                c.here()
                c.add(v.tensor_tensor(V[:, b % 2, 0:n, :], xb, cols(9, t0, n), ALU.mult))
                split(V[:, b % 2, 0:n, :], 1, t0, n)
            general_hop(11)
            for b, (t0, n) in enumerate(BL):
                s_ = sums(11, b, True)
                v.wait_ge(s_gh, 11 * NB + NB + b - 1 + (b == 0))
                c.add(v.tensor_tensor(V[:, b % 2, 0:n, :], s_, cols(10, t0, n), ALU.mult))
                split(V[:, b % 2, 0:n, :], 0, t0, n)
            general_hop(12)
            for b in range(NB + 2):
                if b < NB:
                    t0, n = BL[b]
                    s_ = sums(12, b, False)
                    if b >= 2:
                        v.wait_ge(s_m7, NB + b - 1)
                    v.tensor_tensor(z[:, b % 2, 0:n, 0:D], s_, cols(5, t0, n), ALU.mult).then_inc(s_o, 1)
                if b >= 2:
                    t0, n = BL[b - 2]
                    v.wait_ge(s_y, NB + b - 1)
                    v.wait_ge(s_xc, 9 * NB + b - 1)
                    v.tensor_tensor(V[:, b % 2, 0:n, :], bank[:, b - 2, 0:n * D].rearrange("p (t d) -> p t d", d=D), xc[:, b % 2, 0:n, :], ALU.add).then_inc(s_xcu, 1)
                    v.wait_ge(s_xcu, 9 * NB + b - 1 + 2)
                    norm(2 * NB + b - 2, V[:, b % 2, 0:n, :], n, xs[:, t0:t0 + n, :]).then_inc(s_x3, 1)
            for b, (t0, n) in enumerate(BL):
                v.wait_ge(s_asad, b + 1)
                c.add(v.tensor_copy(asad[:, :, :, t0:t0 + n].rearrange("p e h t -> p (e h) t"), bank[:, b, 0:n * 2 * H].rearrange("p (t e) -> p e t", e=2 * H)))
            c.here()
            c.add(v.tensor_reduce(amax[:, 0, 0:H], asad[:, 0], AX, ALU.max))
            c.add(v.tensor_reduce(amax[:, 0, H:2 * H], asad[:, 0], AX, ALU.min))
            c.here()
            v.tensor_scalar(amax[:, 0, H:2 * H], amax[:, 0, H:2 * H], -1.0, None, ALU.mult).then_inc(s_am, 1)
            v.wait_ge(s_A, 1)
            c.add(v.tensor_tensor(chk1[:, 0:H], amax[0:1, 1, 0:H], amax[0:1, 1, H:2 * H], ALU.add))
            c.here()
            c.add(v.tensor_reduce(chk1[:, 4:5], chk1[:, 0:H], AX, ALU.max))
            v.wait_ge(s_wsqs, 1)
            c.add(v.tensor_reduce(chk1[:, 5:6], bank[0:1, 7, 256:512], AX, ALU.max))
            c.here()
            c.add(v.tensor_scalar(chk1[:, 6:7], chk1[:, 4:5], WIDEST, None, ALU.is_le))
            c.add(v.tensor_scalar(chk1[:, 7:8], chk1[:, 5:6], 900.0, None, ALU.is_le))
            c.here()
            c.add(v.tensor_tensor(chk1[:, 5:6], chk1[:, 6:7], chk1[:, 7:8], ALU.mult))
            c.here()
            c.add(v.tensor_tensor(chk1[:, 4:5], chk1[:, 5:6], flag[:, 0:1], ALU.mult))
            c.here()
            v.tensor_copy(flag[:, 1:2], chk1[:, 4:5]).then_inc(s_flag3, 1)
            v.wait_ge(s_flag3, 1)
            dense3 = v.value_load(flag[0:1, 1:2], min_val=0, max_val=1)
            main, c = c, Count(v, s_v3)
            with v.If(dense3 == 1):
                v.wait_ge(s_agg, 13 * NB)
                v.wait_ge(s_cst, 4)
                for t in range(T):
                    v.tensor_tensor(C[:, t, t * P:(t + 1) * P], C[:, t, t * P:(t + 1) * P], ident16[:], ALU.add).then_inc(s_selfl, 1)
                Ab = amax[:, 1, 0:H, None].to_broadcast([P, H, T])
                c.add(v.tensor_copy(heads[:, :, 0, :], asad[:, 0]))
                c.add(v.tensor_tensor(heads[:, :, 1, :], asad[:, 0], Ab, ALU.subtract))
                c.add(v.tensor_tensor(heads[:, :, 4, :], asad[:, 1], Ab, ALU.add))
                c.here()
                c.add(v.tensor_scalar(heads[:, :, 2, :], heads[:, :, 1, :], 0.2, None, ALU.mult))
                c.add(v.tensor_scalar(heads[:, :, 3, :], heads[:, :, 4, :], 0.2, None, ALU.mult))
                c.here()
                c.add(v.tensor_tensor(asad[:, 1], heads[:, :, 4, :], heads[:, :, 3, :], ALU.max))
                c.here()
                c.add(v.tensor_tensor(asad[:, 0], heads[:, :, 3, :], asad[:, 1], ALU.subtract))
                c.here()
                c.add(v.tensor_tensor(heads[:, :, 3, :], heads[:, :, 4, :], asad[:, 1], ALU.subtract))
                c.here()
                v.tensor_copy(heads[:, :, 4, :], asad[:, 0]).then_inc(s_arg, 1)
                v.wait_ge(s_exp, 1)
                c.add(v.memset(acc[:], 0.0))
                v.tensor_scalar(heads[:, :, 1:3, :], heads[:, :, 1:3, :], XS * LO, None, ALU.mult).then_inc(s_heads, 1)
                c.here()
                v.wait_ge(s_selfl, T)
                v.wait_ge(s_heads, 1)
                v.sem_inc(s_ring, 1)
                v.sem_inc(s_post, 1)
                with v.Fori(0, H) as h:
                    c.loop(h, 1 + 2 * T + 2 * NB)
                    v.wait_ge(s_post, h * NB + 1)
                    v.tensor_copy(hd[:, 0:5, :], heads[:, bass.ds(h, 1), :, :].rearrange("p o a t -> p (o a) t")).then_inc(s_hd, 1)
                    v.wait_ge(s_hd, h + 1)
                    v.tensor_scalar(hd[:, 5, :], hd[:, 0, :], STEEP, None, ALU.mult).then_inc(s_steep, 1)
                    Fe = F[:].rearrange("p t (e c) -> p e t c", e=2)
                    c.add(v.tensor_scalar(Fe[:, :, :, D], hd[:, 1:3, :], 1.0 / LO, None, ALU.mult))
                    c.here()
                    v.scalar_tensor_tensor(Fe[:, :, :, S1 + D], Fe[:, :, :, D], -LO, hd[:, 1:3, :], ALU.mult, ALU.add).then_inc(s_F, 1)
                    for b in range(NB + 1):
                        if b < NB:
                            t0, n = BL[b]
                            v.wait_ge(s_xw, h * NB + (b + 1))
                            if b >= 2:
                                v.wait_ge(s_F, h * (2 * NB + 1) + (1 + 2 * (b - 1)))
                            for e in range(2):
                                v.tensor_tensor((Vg, Vd)[e][:, b % 2, 0:n, 0:D], bank[:, 7 - 3 * (b % 2), 0:n * D].rearrange("p (t d) -> p t d", d=D), hd[:, 1 + e, t0:t0 + n, None].to_broadcast([P, n, D]), ALU.mult).then_inc(s_vg, 1)
                        if b >= 1:
                            t0, n = BL[b - 1]
                            for e in range(2):
                                v.wait_ge(s_vhi, h * (2 * NB) + (2 * (b - 1) + e + 1))
                                o = 2 * S1 * e
                                v.scalar_tensor_tensor(F[:, t0:t0 + n, o + S1:o + S1 + D], F[:, t0:t0 + n, o:o + D], -LO, (Vg, Vd)[e][:, (b - 1) % 2, 0:n, 0:D], ALU.mult, ALU.add).then_inc(s_F, 1)

                    def post(b):
                        t0, n = BL[b]
                        for jj in range(n):
                            t = t0 + jj
                            v.wait_ge(s_c2, h * (2 * T) + (2 * t + 2))
                            v.tensor_tensor(c2[:, jj], c2[:, jj], bank[:, t % RB, 2 * S1:4 * S1], ALU.subtract).then_inc(s_ring, 1)
                            v.wait_ge(s_ring, h * T + (t + 2))
                            c.add(v.scalar_tensor_tensor(r1[:, jj], c2[:, jj], hd[:, 4, t:t + 1], r1[:, jj], ALU.mult, ALU.add))
                        c.here()
                        c.add(v.scalar_tensor_tensor(q[:, 0:n, :], r1[:, 0:n, S1:2 * S1], 1.0 / LO, r1[:, 0:n, 0:S1], ALU.mult, ALU.add))
                        c.here()
                        c.add(v.tensor_scalar(rd[:, 0:n], q[:, 0:n, D], 1e-16 * XS, float(H), ALU.add, ALU.mult))
                        c.here()
                        c.add(v.reciprocal(rd[:, 0:n], rd[:, 0:n]))
                        c.here()
                        for jj in range(n):
                            last = v.scalar_tensor_tensor(acc[:, t0 + jj, :], q[:, jj, 0:D], rd[:, jj:jj + 1], acc[:, t0 + jj, :], ALU.mult, ALU.add)
                            if jj < n - 1:
                                c.add(last)
                        last.then_inc(s_post, 1)

                    for b, (t0, n) in enumerate(BL):
                        for t in range(T):
                            mi = b * T + t
                            if t == RB - 1 and b >= 1:
                                post(b - 1)
                            v.wait_ge(s_Mu, h * (NB * T) + (mi + 1))
                            if by_act(b, t):
                                v.wait_ge(s_step, h * STEPS + sum(by_act(b_, t__) for b_ in range(b + 1) for t__ in range(T if b_ < b else t + 1)))
                                v.tensor_tensor(Mr[:, mi % RB, 0:n * P], Mr[:, mi % RB, 0:n * P], C[:, t, t0 * P:(t0 + n) * P], ALU.mult).then_inc(s_M, 1)
                            else:
                                v.wait_ge(s_nads, h * NB + (b + 1))
                                v.scalar_tensor_tensor(Mr[:, mi % RB, 0:n * P], nadS[:, 0:n * P], hd[:, 0, t:t + 1], C[:, t, t0 * P:(t0 + n) * P], ALU.is_lt, ALU.mult).then_inc(s_M, 1)
                    post(NB - 1)
                    c.end(H)
                v.wait_ge(s_post, H * NB + 1)
            with v.Else():
                v.wait_ge(g_cst3, 5)
                x_ = Count(v, g_vX)
                for t in range(T):
                    v.wait_ge(g_xw, t + 1)
                    v.tensor_copy(g_tabs[:, t, 0:H * D], bank[:, t % 2, 0:H * D]).then_inc(g_xwt, 1)
                x_.add(v.tensor_copy(g_nm, asad[:, 0].rearrange("p h t -> p t h")))
                x_.add(v.tensor_copy(g_tabd[:, :, H:2 * H], asad[:, 1].rearrange("p h t -> p t h")))
                v.wait_ge(g_xwt, T)
                v.tensor_copy(g_tabs[:, :, H * D:GS], asad[:, 0].rearrange("p h t -> p t h")).then_inc(g_tabs_r, 1)
                x_.here()
                with v.Fori(0, GC) as ch:
                    v.wait_ge(g_load3, ch * 16 + 16)
                    v.tensor_copy(g_sd[0:GE, 1:2], g_raw[0:GE, 1:2]).then_inc(g_R_r, 1)
                    v.wait_ge(g_Rp, ch + 1)
                    v.tensor_copy(g_R, bank[:, 0, 0:H * GE].rearrange("p (h e) -> p h e", h=H)).then_inc(g_vX, 1)
                    v.tensor_copy(g_D, bank[:, 1, 0:GE]).then_inc(g_vX, 1)
                    v.wait_ge(g_vX, ch * 2 + 4)
                    v.sem_inc(g_pad, 1)
                    with v.Fori(0, T) as t:
                        v.wait_ge(g_vM, ch * (4 * T) + (t * 4 + 1))
                        v.tensor_scalar(g_pen, g_D, g_jid[:, bass.ds(t, 1)], -BIG, ALU.not_equal, ALU.mult).then_inc(g_vM, 1)
                        v.wait_ge(g_vM, ch * (4 * T) + (t * 4 + 2))
                        v.tensor_tensor(g_val, g_R, g_pen[:, None, :].to_broadcast([P, H, GE]), ALU.add).then_inc(g_vM, 1)
                        v.wait_ge(g_vM, ch * (4 * T) + (t * 4 + 3))
                        v.tensor_reduce(g_mx, g_val, AX, ALU.max).then_inc(g_vM, 1)
                        v.wait_ge(g_vM, ch * (4 * T) + (t * 4 + 4))
                        v.tensor_tensor(g_nm[:, bass.ds(t, 1), :], g_nm[:, bass.ds(t, 1), :], g_mx[:, None, :], ALU.max).then_inc(g_vM, 1)
                    v.wait_ge(g_vM, ch * (4 * T) + (4 * T + 1))
                    v.sem_inc(g_mxd, 1)
                y_ = Count(v, g_vS)
                ad_ = g_tabd[:, :, H:2 * H]
                y_.add(v.tensor_tensor(g_ws[:, 0], g_nm, ad_, ALU.add))
                y_.add(v.tensor_tensor(g_ws[:, 1], g_tabs[:, :, H * D:GS], ad_, ALU.add))
                y_.here()
                y_.add(v.scalar_tensor_tensor(g_tabd[:, :, 0:H], g_ws[:, 0], 0.2, g_ws[:, 0], ALU.mult, ALU.max))
                y_.add(v.scalar_tensor_tensor(g_ws[:, 2], g_ws[:, 1], 0.2, g_ws[:, 1], ALU.mult, ALU.max))
                y_.here()
                v.tensor_tensor(g_ws[:, 1], g_ws[:, 2], g_tabd[:, :, 0:H], ALU.subtract).then_inc(g_wa, 1)
                v.sem_inc(g_tabd_r, 1)
                y_.add(v.memset(acc[:], 0.0))
                y_.here()
                v.sem_inc(g_acc, 1)
                v.wait_ge(g_we, 1)
                v.sem_inc(g_vT, 1)
                with v.Fori(0, H) as h:
                    with v.Fori(0, GC) as ch:
                        k_ = h * (6 * GC) + ch * 6
                        v.wait_ge(g_load3, h * (16 * GC) + (ch * 16 + (16 * GC + 16)))
                        v.wait_ge(g_done3, h * GC + (ch + (GC + 1)))
                        v.tensor_copy(g_sd[0:GE, 1:2], g_raw[0:GE, 1:2]).then_inc(g_vT, 1)
                        v.wait_ge(g_gaths, h * (16 * GC) + (ch * 16 + (16 * GC + 16)))
                        v.wait_ge(g_gathd, h * (16 * GC) + (ch * 16 + 16))
                        v.tensor_tensor(g_w[0:GE, 0:H], g_rs[0:GE, H * D:GS], g_rd[0:GE, H:2 * H], ALU.add).then_inc(g_vT, 1)
                        v.wait_ge(g_vT, k_ + 3)
                        v.scalar_tensor_tensor(g_w[0:GE, H:2 * H], g_w[0:GE, 0:H], 0.2, g_w[0:GE, 0:H], ALU.mult, ALU.max).then_inc(g_vT, 1)
                        v.wait_ge(g_vT, k_ + 4)
                        v.tensor_tensor(g_w[0:GE, 2 * H:3 * H], g_w[0:GE, H:2 * H], g_rd[0:GE, 0:H], ALU.subtract).then_inc(g_wa, 1)
                        v.tensor_scalar(g_oh32[0:GE, :], g_iota[0:GE, :], g_sd[0:GE, 1:2], None, ALU.is_equal).then_inc(g_vT, 1)
                        v.wait_ge(g_we, h * GC + (ch + 2))
                        v.tensor_scalar(g_rhs[0:GE, 0:D], g_rs[0:GE, bass.ds(h * D, D)], g_w[0:GE, bass.ds(h + 3 * H, 1)], None, ALU.mult).then_inc(g_vT, 1)
                        v.tensor_copy(g_rhs[0:GE, D:S1], g_w[0:GE, bass.ds(h + 3 * H, 1)]).then_inc(g_vT, 1)
                        v.wait_ge(g_vT, k_ + 7)
                        v.sem_inc(g_oh3, 1)
                    k_ = h * 11 + 1
                    v.wait_ge(g_close3, h + 1)
                    for q_ in range(4):
                        a_, z_ = 7 * q_, min(7 * q_ + 7, T)
                        v.tensor_copy(g_num[:, a_:z_, :], bank[:, q_, 0:(z_ - a_) * S1].rearrange("p (t c) -> p t c", c=S1)).then_inc(g_acc, 1)
                    w_ = g_ws[:, 2, :, bass.ds(h, 1)]
                    v.tensor_tensor(g_t2, g_tabs[:, :, bass.ds(h * D, D)], w_.to_broadcast([P, T, D]), ALU.mult).then_inc(g_acc, 1)
                    v.wait_ge(g_acc, k_ + 5)
                    v.tensor_tensor(g_num[:, :, 0:D], g_num[:, :, 0:D], g_t2, ALU.add).then_inc(g_acc, 1)
                    v.tensor_tensor(g_num[:, :, D:S1], g_num[:, :, D:S1], w_, ALU.add).then_inc(g_acc, 1)
                    v.wait_ge(g_acc, k_ + 7)
                    v.tensor_scalar(g_num[:, :, D:S1], g_num[:, :, D:S1], 1e-16, float(H), ALU.add, ALU.mult).then_inc(g_acc, 1)
                    v.wait_ge(g_acc, k_ + 8)
                    v.reciprocal(g_t2[:, :, 0:1], g_num[:, :, D:S1]).then_inc(g_acc, 1)
                    v.wait_ge(g_acc, k_ + 9)
                    v.tensor_tensor(g_num[:, :, 0:D], g_num[:, :, 0:D], g_t2[:, :, 0:1].to_broadcast([P, T, D]), ALU.mult).then_inc(g_acc, 1)
                    v.wait_ge(g_acc, k_ + 10)
                    v.tensor_tensor(acc[:], acc[:], g_num[:, :, 0:D], ALU.add).then_inc(g_acc, 1)
                    v.wait_ge(g_acc, k_ + 11)
            c = main
            for b, (t0, n) in enumerate(BL):
                c.here()
                c.add(v.tensor_tensor(acc[:, t0:t0 + n, :], acc[:, t0:t0 + n, :], xs[:, t0:t0 + n, :], ALU.add))
                c.here()
                c.add(v.tensor_tensor(acc[:, t0:t0 + n, :], acc[:, t0:t0 + n, :], biases[:, 2:3, :].to_broadcast([P, n, D]), ALU.add))
                norm(3 * NB + b, acc[:, t0:t0 + n, :], n, acc[:, t0:t0 + n, :]).then_inc(s_fin, 1)

        @block.tensor
        def _(pe):
            pe.sem_inc(s_ohused, AGO)
            pe.wait_ge(s_firstf, 1)
            pe.wait_ge(s_ones, 2)
            pe.matmul(pf[:, 0:512], ones[:], first_f[:, 0:512], start=True, stop=True)
            pe.matmul(pf[:, 512:R], ones[:], first_f[:, 512:R], start=True, stop=True).then_inc(s_firstb, 1)
            pe.wait_ge(s_iota, 9)
            pe.wait_ge(s_cst, 4)
            pe.matmul(pdeg[:, 0:T], ident16[:], C[:, 0, NW:NW + T], start=True, stop=False)
            with pe.Fori(0, G // 2) as i:
                for par in range(2):
                    g = i * 2 + par
                    pe.wait_ge(s_keys, g + 1)
                    for w in range(WG):
                        wi = g * WG + w
                        r = w % RING
                        for half in range(2):
                            if w == HALVES[half][0]:
                                pe.wait_ge(s_lo, g * 2 + (half + 1))
                        pe.wait_ge(s_oh, wi + 1)
                        if w in KEYED:
                            pe.wait_ge(s_keyed, g * len(KEYED) + (KEYED.index(w) + 2))
                        pe.wait_ge(s_evict, wi + (1 + AGO - back(w)))
                        for k in range(K):
                            ch = w * K + k
                            pe.matmul(pk[r][:, 0:KEY], ohp[:, r, :, k], ohk[:, r, k], start=k == 0, stop=k == K - 1)
                            pe.matmul(pdeg[:, 0:T], ohp[:, r, :, k], oht[:, par, :, ch], start=False, stop=False)
                            last = pe.matmul(pea[par][0:65, w * W:(w + 1) * W], eahl[:, ch, :], ohj[:, par, :, ch], start=k == 0, stop=k == K - 1)
                        last.then_inc(s_ohused, 1)
                        for _ in range(KEEP):
                            pe.matmul(bank[:, 6, 0:KEY], ident16[:], iota_key[:].rearrange("p t j -> p (t j)"), start=True, stop=True)
            pe.matmul(pdeg[:, 0:T], ident16[:], C[:, 0, NW:NW + T], start=False, stop=True).then_inc(s_deg, 1)

            WL = 15 * 16
            pe.wait_ge(s_w, WL)
            pe.wait_ge(s_eaev, G)
            pe.wait_ge(s_degacc, 1)
            pe.wait_ge(s_cst, 3)
            for t in range(T):
                pe.matmul(bank[:, 7, t:t + 1], eaT[:, t * P:(t + 1) * P], row64[:], start=t == 0, stop=False)
            pe.matmul(bank[:, 7, P:P + D], wlr[:], ident[0:D, 0:D], start=False, stop=True).then_inc(s_t7, 1)

            pe.wait_ge(s_chk, 1)
            pe.matmul(bank[0:1, 7, 256:258], onesP[:], chk[:], start=True, stop=True).then_inc(s_chks, 1)
            pe.wait_ge(s_flag, 1)
            dense = pe.value_load(flag[0:1, 0:1], min_val=0, max_val=1)

            def zeros(banks, cols_, start, sem_=None):
                for b_ in banks:
                    last = pe.matmul(bank[:, b_, 0:cols_], g_zero[0:1, 0:P], g_zero[0:1, 0:cols_], start=start, stop=not start)
                    if sem_ is not None:
                        last.then_inc(sem_, 1)
                return last

            with pe.If(dense == 0):
                pe.wait_ge(g_cst, 5)
                pe.sem_inc(g_done, 1)
                zeros(range(NB), 512, True)
                zeros([7], T, True)
                with pe.Fori(0, GC) as ch:
                    pe.wait_ge(g_oh, ch + 1)
                    for b, (t0, n) in enumerate(BL):
                        pe.matmul(bank[0:S1, b, 0:n * P], g_ea[0:GE, 0:S1], g_ohd[0:GE, t0 * P:(t0 + n) * P], start=False, stop=False)
                    for t in range(T):
                        last = pe.matmul(bank[:, 7, t:t + 1], g_ohs[0:GE, t * P:(t + 1) * P], g_one[0:GE, 0:1], start=False, stop=False)
                    last.then_inc(g_done, 1)
                zeros(range(NB), 512, False)
                zeros([7], T, False).then_inc(g_close, 1)
                pe.wait_ge(g_taken, NB + 1)
                for t in range(T):
                    last = pe.matmul(bank[:, 7, t:t + 1], eaT[:, t * P:(t + 1) * P], row64[:], start=t == 0, stop=t == T - 1)
                last.then_inc(g_close, 1)
            pe.wait_ge(s_wsq, 1)
            pe.wait_ge(s_nrm, 1)
            pe.matmul(bank[0:1, 7, 256:512], onesP[0:D, :], att[:, 1].rearrange("p h d -> p (h d)"), start=True, stop=True).then_inc(s_wsqs, 1)

            def hop(kk, par, which, after=None):
                with pe.If(dense == 1):
                    dense_hop(kk, par, after)
                with pe.Else():
                    pe.wait_ge(s_free, kk * NB + NB)
                    pe.wait_ge(s_gh, kk * NB + NB)
                    zeros(range(NB), 512, True)
                    with pe.Fori(0, GC) as ch:
                        pe.wait_ge(g_oh, (kk + 1) * GC + (ch + 1))
                        pe.wait_ge(which[0], which[1] * (16 * GC) + (ch * 16 + 16))
                        for t in range(T):
                            last = pe.matmul(bank[:, t // 4, (t % 4) * 2 * D:(t % 4 + 1) * 2 * D], g_ohd[0:GE, t * P:(t + 1) * P], g_rows[0:GE, :], start=False, stop=False)
                        last.then_inc(g_done, 1)
                    zeros(range(NB), 512, False, s_agg)
                    if after:
                        for b in range(NB):
                            after(b)

            def dense_hop(kk, par, after):
                for b, (t0, n) in enumerate(BL):
                    pe.wait_ge(s_free, kk * NB + (b + 1))
                    early = T - 5 if b == 0 else T
                    if b == 0:
                        pe.wait_ge(s_gh, kk * NB + (NB - 2))
                    for lo_, hi_ in ((0, early), (early, T)):
                        if lo_ == hi_:
                            continue
                        if lo_:
                            pe.wait_ge(s_gh, kk * NB + NB)
                        for jj in range(n):
                            for t in range(lo_, hi_):
                                last = pe.matmul(bank[:, b, jj * 2 * D:(jj + 1) * 2 * D], C[:, t, (t0 + jj) * P:(t0 + jj + 1) * P], GH[:, par, t, :],
                                                 start=t == 0 and jj == 0, stop=jj == n - 1 and t == T - 1)
                    last.then_inc(s_agg, 1)
                    if after:
                        after(b)

            with pe.Fori(0, 4) as i:
                for par in range(2):
                    hop(i * 2 + par, par, gathered(par, i))
            hop(8, 0, gathered(8))
            hop(9, 1, gathered(9))

            def l1_sum(b):
                t0, n = BL[b]
                pe.wait_ge(s_o, b + 1)
                if b >= 1:
                    pe.wait_ge(s_oT, b)
                pe.matmul(bank[0:D, 7, 0:n * P], weS[:], eaT[:, t0 * P:(t0 + n) * P], start=True, stop=False)
                for j in range(n):
                    last = pe.matmul(bank[0:D, 7, j * P:(j + 1) * P], z[:, b % 2, j, 0:D], ident[:], start=False, stop=j == n - 1)
                last.then_inc(s_m7, 1)

            def l1_up(b):
                t0, n = BL[b]
                pe.wait_ge(s_oT, b + 1)
                pe.matmul(bank[0:D, b, 0:n * P], w1[:], zT[0:D, b % 2, 0:n * P], start=True, stop=True).then_inc(s_h, 1)

            def after1(b):
                if b >= 1:
                    l1_sum(b - 1)
                if b >= 2:
                    l1_up(b - 2)
            hop(10, 0, gathered(10), after1)
            l1_sum(NB - 1)
            l1_up(NB - 2)
            l1_up(NB - 1)
            pe.wait_ge(s_row1, 1)
            for b, (t0, n) in enumerate(BL):
                pe.wait_ge(s_relu, b + 1)
                for j in range(n):
                    last = pe.matmul(bank[:, b, j * D:(j + 1) * D], eaT[:, (t0 + j) * P:(t0 + j + 1) * P], w2[:], start=j == 0, stop=j == n - 1)
                last.then_inc(s_y, 1)
            hop(11, 1, gathered(11))

            def l2_turn(b):
                n = BL[b][1]
                pe.wait_ge(s_o, NB + b + 1)
                pe.wait_ge(s_xc, 9 * NB + b + 1)
                pe.wait_ge(s_oT, NB + b)
                for j in range(n):
                    last = pe.matmul(bank[:, 7, j * P:(j + 1) * P], z[:, b % 2, j, :], ident[:], start=j == 0, stop=j == n - 1)
                last.then_inc(s_m7, 1)

            def l2_down(b):
                n = BL[b][1]
                pe.wait_ge(s_oT, NB + b + 1)
                for j in range(n):
                    last = pe.matmul(bank[:, b, j * D:(j + 1) * D], zT[:, b % 2, j * P:(j + 1) * P], wlrT[:], start=j == 0, stop=j == n - 1)
                last.then_inc(s_y, 1)

            def after2(b):
                if b >= 1:
                    l2_turn(b - 1)
                if b >= 2:
                    l2_down(b - 2)
            hop(12, 0, gathered(12), after2)
            l2_turn(NB - 1)
            l2_down(NB - 2)
            l2_down(NB - 1)
            pe.wait_ge(s_t7r, 1)
            for b in range(NB + 1):
                if b < NB:
                    t0, n = BL[b]
                    pe.wait_ge(s_x3, b + 1)
                    pe.wait_ge(s_oT, 2 * NB + b)
                    for j in range(n):
                        last = pe.matmul(bank[0:D, 7, j * P:(j + 1) * P], xs[:, t0 + j, :], ident[:], start=j == 0, stop=j == n - 1)
                    last.then_inc(s_m7, 1)
                if b >= 1:
                    t0, n = BL[b - 1]
                    pe.wait_ge(s_oT, 2 * NB + b)
                    for j in range(n):
                        last = pe.matmul(bank[:, b - 1, j * 2 * H:(j + 1) * 2 * H], eaT[0:D, (t0 + j) * P:(t0 + j + 1) * P], wa[:].rearrange("p e h -> p (e h)"), start=j == 0, stop=j == n - 1)
                    last.then_inc(s_asad, 1)
            pe.wait_ge(s_flag3, 1)
            dense3 = pe.value_load(flag[0:1, 1:2], min_val=0, max_val=1)
            with pe.If(dense3 == 1):
                pe.sem_inc(s_Mu, RB)
                pe.sem_inc(s_nad, 1)
                with pe.Fori(0, H) as h:
                    pe.wait_ge(s_wh, h * 2 + 2)
                    for b, (t0, n) in enumerate(BL):
                        if b == 1:
                            pe.wait_ge(s_ring, h * T + 1)
                        if b >= 2:
                            pe.wait_ge(s_vg, h * (2 * NB) + 2 * (b - 1))
                        for j in range(n):
                            last = pe.matmul(bank[:, 7 - 3 * (b % 2), j * D:(j + 1) * D], eaT[0:D, (t0 + j) * P:(t0 + j + 1) * P], wgh[:], start=j == 0, stop=j == n - 1)
                        last.then_inc(s_xw, 1)

                    def nad(b):
                        t0, n = BL[b]
                        pe.matmul(bank[:, 5 + b % 2, 0:n * P], wadb[:], eaT[0:D, t0 * P:(t0 + n) * P], start=True, stop=True).then_inc(s_nad, 1)
                    nad(0)
                    nad(1)
                    for b, (t0, n) in enumerate(BL):
                        for jj in range(n):
                            t_ = t0 + jj
                            if b == 0 and jj == 0:
                                pe.wait_ge(s_F, h * (2 * NB + 1) + (2 * NB + 1))
                            if t_ >= RB:
                                pe.wait_ge(s_ring, h * T + (t_ - RB + 2))
                            for t in range(T):
                                pe.matmul(bank[:, t_ % RB, 4 * S1:6 * S1], C[:, t, t_ * P:(t_ + 1) * P], F[:, t, 2 * S1:4 * S1], start=t == 0, stop=t == T - 1)
                        for t in range(T):
                            mi = b * T + t
                            pe.wait_ge(s_M, h * (NB * T) + (mi + 1))
                            for jj in range(n):
                                last = pe.matmul(bank[:, (t0 + jj) % RB, 0:4 * S1], Mr[:, mi % RB, jj * P:(jj + 1) * P], F[:, t, :], start=t == 0, stop=t == T - 1)
                            last.then_inc(s_Mu, 1)
                        if b + 2 < NB:
                            nad(b + 2)
            with pe.Else():
                for t in range(T):
                    if t >= 2:
                        pe.wait_ge(g_xwt, t - 1)
                    pe.matmul(bank[:, t % 2, 0:H * D], eaT[0:D, t * P:(t + 1) * P], wg[:].rearrange("k h d -> k (h d)"), start=True, stop=True).then_inc(g_xw, 1)
                pe.wait_ge(g_xwt, T)
                pe.wait_ge(g_cst3, 5)
                pe.sem_inc(g_done3, 1)
                pe.sem_inc(g_vM, 1)
                with pe.Fori(0, GC) as ch:
                    pe.wait_ge(g_gaths, ch * 16 + 16)
                    pe.wait_ge(g_R_r, ch + 1)
                    for h in range(H):
                        pe.matmul(bank[:, 0, h * GE:(h + 1) * GE], g_rs[0:GE, H * D + h:H * D + h + 1].to_broadcast([GE, P]), ident[0:GE, 0:GE], start=h == 0, stop=h == H - 1)
                    pe.matmul(bank[:, 1, 0:GE], g_sd[0:GE, 1:2].to_broadcast([GE, P]), ident[0:GE, 0:GE], start=True, stop=True).then_inc(g_Rp, 1)
                    pe.wait_ge(g_mxd, ch + 1)
                    pe.sem_inc(g_done3, 1)
                with pe.Fori(0, H) as h:
                    pe.wait_ge(g_acc, h * 11 + 1)
                    zeros(range(4), 7 * S1, True)
                    with pe.Fori(0, GC) as ch:
                        pe.wait_ge(g_oh3, h * GC + (ch + 1))
                        for t in range(T):
                            last = pe.matmul(bank[:, t // 7, (t % 7) * S1:(t % 7 + 1) * S1], g_oh32[0:GE, t * P:(t + 1) * P], g_rhs[0:GE, :], start=False, stop=False)
                        last.then_inc(g_done3, 1)
                    zeros(range(3), 7 * S1, False)
                    zeros([3], 7 * S1, False).then_inc(g_close3, 1)


_INS = ["L1_gnn_We", "L1_gnn_be", "L1_gnn_W1", "L1_gnn_b1", "L1_gnn_gamma", "L1_gnn_beta", "L1_gnn_W2", "L1_gnn_b2",
        "L2_gnn_W", "L2_gnn_b", "L2_gnn_Wr", "L2_gnn_br", "L3_gnn_W", "L3_gnn_att_src", "L3_gnn_att_dst", "L3_gnn_bias"]
_OUTS = [((3125, 64), "float32")]


def kernel(**inputs):
    import numpy as _np
    import concourse.bacc as _bacc
    from concourse import mybir as _mybir
    from concourse.bass_utils import run_bass_kernel_spmd as _run
    nc = _bacc.Bacc("TRN2", target_bir_lowering=False, num_devices=1, dynamic_dma_scratch_size=4096)
    arrays, args = {}, []
    packed = {k: _np.ascontiguousarray(inputs[k]) for k in ("x", "dst")}
    packed["edges"] = _np.concatenate([_np.asarray(inputs["src"])[:, None], _np.asarray(inputs["dst"])[:, None],
                                       _np.asarray(inputs["edge_attr_32"]).view(_np.int32)], axis=1)
    packed.update({k: _np.ascontiguousarray(inputs[k]) for k in _INS})
    for name, a in packed.items():
        arrays[f"in_{name}_dram"] = a
        args.append(nc.dram_tensor(f"in_{name}_dram", a.shape, _mybir.dt.from_np(a.dtype), kind="ExternalInput").ap())
    for i, (shape, dtype) in enumerate(_OUTS):
        dt = _mybir.dt.from_np(_np.dtype(dtype))
        args.append(nc.dram_tensor(f"out_{i}_dram", shape, dt, kind="ExternalOutput").ap())
    gnn_kernel(nc, *args)
    r = _run(nc, [arrays], core_ids=[0])
    got = tuple(r.results[0][f"out_{i}_dram"] for i in range(len(_OUTS)))
    return got[0]
```
